# Optimizing a Trainium2 kernel written in Bass

```python
import numpy as np
import jax
import jax.numpy as jnp

def _softmax(x, axis=-1):
    return jax.nn.softmax(x, axis=axis)

def _gelu(x):
    return jax.nn.gelu(x, approximate=True)

def _silu(x):
    return jax.nn.silu(x)

def _sigmoid(x):
    return jax.nn.sigmoid(x)

def _layernorm(x, axis=-1, eps=1e-05):
    m = jnp.mean(x, axis=axis, keepdims=True)
    v = jnp.var(x, axis=axis, keepdims=True)
    return (x - m) / jnp.sqrt(v + eps)

def _scatter_add(tgt, idx, src, axis=0):
    return tgt.at[idx].add(src)

def _segment_sum(src, seg, n):
    return jax.ops.segment_sum(src, seg, n)
kernel_name = 'mk_perceiver_d1_seqx_r4_c975f2'

def setup_inputs(seed: int=0):
    np.random.seed(seed)
    _w = jnp.asarray

    def _rec_inputs():
        import jax
        import jax.numpy as jnp
        _rk = jax.random.key(seed)
        x = -0.0003929 + 0.9999 * jax.random.normal(jax.random.fold_in(_rk, 1), (1, 256, 256), jnp.float32)
        _lenS = 256 - jax.random.randint(jax.random.fold_in(_rk, 7), (1,), 0, max(1, 256 // 4) + 1, jnp.int32)
        _lenS2 = 4096 - jax.random.randint(jax.random.fold_in(_rk, 8), (1,), 0, max(1, 4096 // 4) + 1, jnp.int32)
        _ctx_1024P = jax.random.normal(jax.random.fold_in(_rk, 11), (1, 16, 256), jnp.float32)
        _ctx_1024c = jax.random.dirichlet(jax.random.fold_in(_rk, 511), 0.3 * jnp.ones((16,), jnp.float32), (1, 4096))
        _ctx_1024t = jnp.einsum('bsk,bkd->bsd', _ctx_1024c, _ctx_1024P)
        _ctx_1024t = _ctx_1024t * jax.lax.rsqrt(jnp.mean(jnp.square(_ctx_1024t)) + 1e-12) * 0.953939
        ctx_1024 = 2.81802e-05 + 1.00001 * (_ctx_1024t + 0.3 * jax.random.normal(jax.random.fold_in(_rk, 611), (1, 4096, 256), jnp.float32))
        return (x, ctx_1024)
    x, ctx_1024 = _rec_inputs()

    def _L0_xattn_setup():
        import jax, jax.numpy as jnp
        import numpy as np
        B, SQ, SV, D = (8, 512, 512, 256)
        key = jax.random.key(seed)
        kq, kv = jax.random.split(key)
        query = jax.random.normal(kq, (B, SQ, D), dtype=jnp.float32)
        value = jax.random.normal(kv, (B, SV, D), dtype=jnp.float32)
        return {'query': query, 'value': value}
    _L0_xattn_all = _L0_xattn_setup()
    _L0_xattn_in = {k: v for k, v in _L0_xattn_all.items() if k in ()}
    del _L0_xattn_all

    def _L0_attn_setup():
        import math
        import jax, jax.numpy as jnp
        import numpy as np
        N_EMBD = 256
        N_HEAD = 16
        HEAD_DIM = N_EMBD // N_HEAD

        def alibi_slopes(n_heads):
            start = 2.0 ** (-2.0 ** (-(math.log2(n_heads) - 3)))
            return np.array([start * start ** i for i in range(n_heads)], dtype=np.float32)
        key = jax.random.key(seed)
        k1, k2, k3 = jax.random.split(key, 3)
        B, T, C = (2, 512, N_EMBD)
        x = jax.random.normal(k1, (B, T, C), dtype=jnp.float32)
        w_attn = jax.random.normal(k2, (3 * C, C), dtype=jnp.float32) * (1.0 / math.sqrt(C))
        w_proj = jax.random.normal(k3, (C, C), dtype=jnp.float32) * (1.0 / math.sqrt(C))
        return {'x': x, 'w_attn': w_attn, 'w_proj': w_proj}
    _L0_attn_all = _L0_attn_setup()
    _L0_attn_in = {k: v for k, v in _L0_attn_all.items() if k in ('w_attn', 'w_proj')}
    del _L0_attn_all

    def _L0_ffn_setup():
        import jax, jax.numpy as jnp
        import numpy as np
        B, T, C, H, E = (4, 512, 256, 512, 8)
        CAPACITY_FACTOR = 1.0
        key = jax.random.key(seed)
        ks = jax.random.split(key, 5)
        scale = 0.02
        return {'x': jax.random.normal(ks[0], (B, T, C), dtype=jnp.float32), 'Wg': jax.random.normal(ks[1], (E, C), dtype=jnp.float32) * scale, 'W1': jax.random.normal(ks[2], (E, H, C), dtype=jnp.float32) * scale, 'W2': jax.random.normal(ks[3], (E, C, H), dtype=jnp.float32) * scale, 'W3': jax.random.normal(ks[4], (E, H, C), dtype=jnp.float32) * scale}
    _L0_ffn_all = _L0_ffn_setup()
    _L0_ffn_in = {k: v for k, v in _L0_ffn_all.items() if k in ('Wg', 'W1', 'W2', 'W3')}
    del _L0_ffn_all
    return {'x': x, 'ctx_1024': ctx_1024, 'L0_attn_w_attn': _L0_attn_in['w_attn'], 'L0_attn_w_proj': _L0_attn_in['w_proj'], 'L0_ffn_Wg': _L0_ffn_in['Wg'], 'L0_ffn_W1': _L0_ffn_in['W1'], 'L0_ffn_W2': _L0_ffn_in['W2'], 'L0_ffn_W3': _L0_ffn_in['W3']}

def reference(x, ctx_1024, L0_attn_w_attn, L0_attn_w_proj, L0_ffn_Wg, L0_ffn_W1, L0_ffn_W2, L0_ffn_W3):
    import jax
    import jax.numpy as jnp

    def _L0_xattn_ref(query, value):
        import jax, jax.numpy as jnp
        import numpy as np
        B, SQ, SV, D = (8, 512, 512, 256)
        scores = jnp.einsum('bqd,bkd->bqk', query, value)
        distribution = jax.nn.softmax(scores, axis=-1)
        attention = jnp.einsum('bqk,bkd->bqd', distribution, value)
        return attention

    def _L0_attn_ref(x, w_attn, w_proj):
        import math
        import jax, jax.numpy as jnp
        import numpy as np
        N_EMBD = 256
        N_HEAD = 16
        HEAD_DIM = N_EMBD // N_HEAD

        def alibi_slopes(n_heads):
            start = 2.0 ** (-2.0 ** (-(math.log2(n_heads) - 3)))
            return np.array([start * start ** i for i in range(n_heads)], dtype=np.float32)
        B, T, C = x.shape
        H, D = (N_HEAD, HEAD_DIM)
        qkv = x @ w_attn.T
        q, k, v = jnp.split(qkv, 3, axis=-1)
        q = q.reshape(B, T, H, D).transpose(0, 2, 1, 3)
        k = k.reshape(B, T, H, D).transpose(0, 2, 1, 3)
        v = v.reshape(B, T, H, D).transpose(0, 2, 1, 3)
        att = jnp.einsum('bhqd,bhkd->bhqk', q, k) * (1.0 / math.sqrt(D))
        pos = jnp.arange(T)
        rel = pos[None, :] - pos[:, None]
        slopes = jnp.asarray(alibi_slopes(H))[:, None, None]
        causal = rel <= 0
        bias = jnp.where(causal, slopes * rel, -jnp.inf)
        att = att + bias[None]
        att = jax.nn.softmax(att, axis=-1)
        y = jnp.einsum('bhqk,bhkd->bhqd', att, v)
        y = y.transpose(0, 2, 1, 3).reshape(B, T, C)
        return y @ w_proj.T

    def _L0_ffn_ref(x, Wg, W1, W2, W3):
        import jax, jax.numpy as jnp
        import numpy as np
        B, T, C, H, E = (4, 512, 256, 512, 8)
        CAPACITY_FACTOR = 1.0
        b, t, c = x.shape
        e = Wg.shape[0]
        n = b * t
        capacity = max(1, int(CAPACITY_FACTOR * n / e))
        x_flat = x.reshape(n, c)
        scores = (x_flat @ Wg.T).T
        top_vals, token_idx = jax.lax.top_k(scores, capacity)
        token_w = jax.nn.softmax(top_vals, axis=-1)
        xg = x_flat[token_idx]
        h = jax.nn.silu(jnp.einsum('eic,ehc->eih', xg, W1)) * jnp.einsum('eic,ehc->eih', xg, W3)
        y = jnp.einsum('eih,ech->eic', h, W2) * token_w[..., None]
        out = jnp.zeros_like(x_flat).at[token_idx.reshape(-1)].add(y.reshape(-1, c))
        return out.reshape(b, t, c)
    x = x + _L0_xattn_ref(_layernorm(x, axis=-1), ctx_1024)
    x = x + _L0_attn_ref(_layernorm(x, axis=-1), L0_attn_w_attn, L0_attn_w_proj)
    x = x + _L0_ffn_ref(_layernorm(x, axis=-1), L0_ffn_Wg, L0_ffn_W1, L0_ffn_W2, L0_ffn_W3)
    return x

_drawn_inputs = setup_inputs


def setup_inputs(seed=0):
    import zlib

    import numpy as np

    out = dict(_drawn_inputs(seed))
    spreads = {}
    factors = {'L0_ffn_Wg': 8.0, 'L0_ffn_W1': 8.0, 'L0_ffn_W2': 8.0, 'L0_ffn_W3': 8.0}
    for name, (base, spread) in spreads.items():
        noise = np.random.default_rng([zlib.crc32(name.encode()), seed]).standard_normal(out[name].shape)
        drawn = base * np.exp(spread * noise) if base else spread * noise
        out[name] = jnp.asarray(drawn.astype(out[name].dtype))
    for name, factor in factors.items():
        out[name] = (out[name] * factor).astype(out[name].dtype)
    return out
```

```python
from contextlib import ExitStack

import concourse.bass as bass
import concourse.mybir as mybir

FP32 = mybir.dt.float32
ALU = mybir.AluOpType
ACT = mybir.ActivationFunctionType
AX = mybir.AxisListType

P = 128
T, C, S = 256, 256, 4096
TB, KC = T // P, C // P
CH = 512
NCH = S // CH
NT = CH // P
NH, HD = 16, 16
NG = NH // 4
HPT = P // HD
E, H, CAP = 8, 512, 32
KH = H // P
EG = E // 4
EPS = 1e-5
MASKED = -1e30
TAKEN = -3e38
SLOPES = [2.0 ** (-0.5 * (h + 1)) for h in range(NH)]


def units(n):
    g, kind = n // 3, n % 3
    return (g, 0, range(0, 4), P) if kind == 0 else (g, 1, range(2 * kind - 2, 2 * kind), 2 * P)


NU = 3 * NG


def build(nc, x, ctx_t, ctx_v, w_qkv, w_proj, w_gate, w_up, w_down, out):
    es = ExitStack()
    with es:
        def sb(name, shape):
            return es.enter_context(nc.sbuf_tensor(name, shape, FP32))

        def sem(name):
            return es.enter_context(nc.semaphore(name))

        x_sb = sb("x_sb", [P, TB, C])
        kT = sb("kT", [P, NCH, KC, CH])
        v_sb = sb("v_sb", [P, NCH, NT, C])
        wqkv_sb = sb("wqkv_sb", [P, KC, 3 * C])
        wproj_sb = sb("wproj_sb", [P, NG, C])
        wg_sb = sb("wg_sb", [P, KC, E])
        wup_sb = sb("wup_sb", [P, E, 2, KC, H])
        wdn_sb = sb("wdn_sb", [P, E, KH, C])
        ident = sb("ident", [P, P])
        power = sb("power", [P, 1])
        headmask = sb("headmask", [P, HPT])
        slot_no = sb("slot_no", [P, CAP])
        ones_row = sb("ones_row", [E, T])
        stats = sb("stats", [P, TB, 6])
        meanvar = sb("meanvar", [P, TB, 2])
        vareps = sb("vareps", [P, TB])
        rstd = sb("rstd", [P, TB])
        xn = sb("xn", [P, TB, C])
        xnT = sb("xnT", [P, KC, T])
        negmax = sb("negmax", [P, TB, NCH])
        chunkneg = sb("chunkneg", [P, TB])
        shrink = sb("shrink", [P, TB, NCH])
        rowsum = sb("rowsum", [P, TB, NCH])
        denom = sb("denom", [P, TB])
        rdenom = sb("rdenom", [P, TB])
        acc = sb("acc", [P, TB, C])
        probs_both = sb("probs_both", [P, 2 * TB * CH])
        probs = probs_both[:, 0:TB * CH].rearrange("p (b k) -> p b k", b=TB)
        probsT = probs_both[:, TB * CH:].rearrange("p (b n q) -> p b n q", b=TB, n=NT)
        bias = kT[:, 0:6].rearrange("p a b c -> p (a b c)").rearrange("p (h k) -> p h k", h=NH)
        kM = v_sb[:, 0:4].rearrange("p a b c -> p (a b c)").rearrange("p (h k) -> p h k", h=NH)
        k_plain = v_sb[:, 4].rearrange("p a b -> p (a b)")[:, 0:2 * T].rearrange("p (a t) -> p a t", a=2)
        vaug = v_sb[:, 5:6].rearrange("p a b c -> p (a b c)").rearrange("p (k h d) -> p k h d", k=TB, h=NH)
        biased = probs_both[:, 0:1536].rearrange("p (s k) -> p s k", s=3)
        nmax = sb("nmax", [P, NU, 4])
        aprobs = kT[:, 6:8].rearrange("p a b c -> p (a b c)")[:, 0:1536].rearrange("p (s k) -> p s k", s=3)
        aprobsT = sb("aprobsT", [P, 2, 4, 3, P])
        last_v = v_sb[:, 6:8].rearrange("p a b c -> p (a b c)")
        q_T = last_v[:, 0:2 * T].rearrange("p (m t) -> p m t", m=2)
        y_T = last_v[:, 2 * T:2 * T + NG * T].rearrange("p (g t) -> p g t", g=NG)
        r_T = last_v[:, (2 + NG) * T:(3 + NG) * T]

        scores = sb("scores", [E, T])
        work = sb("work", [E, T])
        top = sb("top", [E, CAP])
        negtop = sb("negtop", [E, 1])
        expd = sb("expd", [E, T])
        taken = sb("taken", [E, T])
        place = sb("place", [E, 2, T])
        wsum = sb("wsum", [E, 1])
        pw = sb("pw", [P, 2, TB, E])
        free = [kT[:, 0:6].rearrange("p a b c -> p (a b c)"), 0]

        def over_bias(size, pattern, **axes):
            part = free[0][:, free[1]:free[1] + size]
            free[1] += size
            return part.rearrange(pattern, **axes)

        onehot = over_bias(TB * E * CAP, "p (b n) -> p b n", b=TB)
        weighted = over_bias(TB * E * CAP, "p (b n) -> p b n", b=TB)
        scatter = over_bias(EG * TB * P, "p (g b t) -> p g b t", g=EG, b=TB)
        xg_T = over_bias(KC * E * CAP, "p (k n) -> p k n", k=KC)
        act = over_bias(EG * H, "p (g h) -> p g h", g=EG)
        h_T = over_bias(EG * KH * P, "p (g k n) -> p g k n", g=EG, k=KH)
        y_e = over_bias(EG * C, "p (g c) -> p g c", g=EG)
        x_out = over_bias(TB * C, "p (b c) -> p b c", b=TB)

        banks = [es.enter_context(nc.psum_tensor(f"bank{i}", [P, 512], FP32)) for i in range(8)]
        s_bank, t_bank, o_bank = banks[0:2], banks[4:6], banks[6:8]
        ln_ps = [banks[2 + b][:, 0:C].rearrange("p (k t) -> p k t", k=KC) for b in range(TB)]
        q_ps = banks[3][:, :].rearrange("p (k t) -> p k t", k=2)
        k_ps = banks[4][:, :].rearrange("p (k t) -> p k t", k=2)
        v_ps = banks[5][:, :].rearrange("p (k c) -> p k c", k=2)
        as_bank = [banks[0], banks[1], banks[6]]
        at_bank = [banks[7], banks[2]]
        y_ps = banks[4][:, 0:T]
        proj_ps = [banks[3][:, 0:C], banks[5][:, 0:C]]

        router_ps = banks[0][0:E, 0:T]
        pw_ps = banks[1][:, 0:2 * TB * E]
        xg_ps = [banks[3][:, 0:E * CAP], banks[2][:, 0:E * CAP]]
        scatter_ps = banks[0][:, :].rearrange("p (g b t) -> p g b t", g=EG, b=TB)
        up_ps = [[banks[4], banks[5]], [banks[6], banks[7]]]
        hT_ps = [banks[1], banks[0]]
        down_ps = [banks[2][:, 0:C], banks[3][:, 0:C]]
        moe_ps = [banks[4][:, 0:C], banks[5][:, 0:C]]

        x_loaded = sem("x_loaded")
        kT_loaded = sem("kT_loaded")
        v_loaded = sem("v_loaded")
        wqkv_loaded = sem("wqkv_loaded")
        wproj_loaded = sem("wproj_loaded")
        wg_loaded = sem("wg_loaded")
        wup_loaded = [sem(f"wup_loaded{g}") for g in range(EG)]
        wdn_loaded = [sem(f"wdn_loaded{g}") for g in range(EG)]
        out_stored = sem("out_stored")
        const_step = sem("const_step")
        ident_ready = sem("ident_ready")
        power_ready = sem("power_ready")
        consts_ready = sem("consts_ready")
        dve_step = sem("dve_step")
        vareps_ready = sem("vareps_ready")
        rstd_ready = sem("rstd_ready")
        xn_ready = sem("xn_ready")
        xnT_in_psum = sem("xnT_in_psum")
        xnT_ready = sem("xnT_ready")
        scores_ready = sem("scores_ready")
        chunkmax_ready = sem("chunkmax_ready")
        negmax_ready = sem("negmax_ready")
        probs_ready = sem("probs_ready")
        shrink_ready = sem("shrink_ready")
        probsT_in_psum = sem("probsT_in_psum")
        probsT_ready = sem("probsT_ready")
        chunk_out_ready = sem("chunk_out_ready")
        denom_ready = sem("denom_ready")
        acc_ready = sem("acc_ready")
        qkv_in_psum = sem("qkv_in_psum")
        q_ready = sem("q_ready")
        k_plain_ready = sem("k_plain_ready")
        vaug_ready = sem("vaug_ready")
        bias_ready = sem("bias_ready")
        bias_step = sem("bias_step")
        vones_ready = sem("vones_ready")
        kM0_ready = sem("kM0_ready")
        kM_ready = sem("kM_ready")
        ascores_ready = sem("ascores_ready")
        biased_ready = sem("biased_ready")
        aprobs_ready = sem("aprobs_ready")
        aprobsT_in_psum = sem("aprobsT_in_psum")
        aprobsT_q0_ready = sem("aprobsT_q0_ready")
        aprobsT_q1_ready = sem("aprobsT_q1_ready")
        y_in_psum = sem("y_in_psum")
        y_T_ready = sem("y_T_ready")
        proj_ready = sem("proj_ready")

        router_in_psum = sem("router_in_psum")
        negtop_ready = sem("negtop_ready")
        expd_ready = sem("expd_ready")
        place_ready = sem("place_ready")
        weight_ready = sem("weight_ready")
        pw_in_psum = sem("pw_in_psum")
        onehot_ready = sem("onehot_ready")
        weighted_ready = sem("weighted_ready")
        xg_in_psum = sem("xg_in_psum")
        xg0_ready = sem("xg0_ready")
        xg1_ready = sem("xg1_ready")
        scatter_in_psum = sem("scatter_in_psum")
        scatter_ready = sem("scatter_ready")
        gate_in_psum = sem("gate_in_psum")
        up_in_psum = sem("up_in_psum")
        silu_ready = sem("silu_ready")
        act_ready = sem("act_ready")
        hT_in_psum = sem("hT_in_psum")
        hT_ready = sem("hT_ready")
        down_in_psum = sem("down_in_psum")
        y_e_ready = sem("y_e_ready")
        moe_in_psum = sem("moe_in_psum")
        x_final = sem("x_final")

        block = es.enter_context(nc.Block())

        @block.sync
        def _(sync):
            sync.dma_start(x_sb[:, :, :], x).then_inc(x_loaded, 16)
            sync.dma_start(kT[:, 0], ctx_t[0]).then_inc(kT_loaded, 16)
            sync.dma_start(v_sb[:, 0], ctx_v[0]).then_inc(v_loaded, 16)
            for i in range(1, NCH):
                sync.wait_ge(kT_loaded, i * 16)
                sync.dma_start(kT[:, i], ctx_t[i]).then_inc(kT_loaded, 16)
                sync.wait_ge(v_loaded, i * 16)
                sync.dma_start(v_sb[:, i], ctx_v[i]).then_inc(v_loaded, 16)
            sync.dma_start(wqkv_sb[:, :, :], w_qkv).then_inc(wqkv_loaded, 16)
            sync.dma_start(wproj_sb[:, :, :], w_proj).then_inc(wproj_loaded, 16)
            sync.dma_start(wg_sb[:, :, :], w_gate).then_inc(wg_loaded, 16)
            for g in range(EG):
                sync.dma_start(wup_sb[:, 4 * g:4 * g + 4], w_up[:, 4 * g:4 * g + 4]).then_inc(wup_loaded[g], 16)
                sync.dma_start(wdn_sb[:, 4 * g:4 * g + 4], w_down[:, 4 * g:4 * g + 4]).then_inc(wdn_loaded[g], 16)
            for b in range(TB):
                sync.wait_ge(x_final, b + 1)
                sync.dma_start(out[:, b], x_out[:, b]).then_inc(out_stored, 16)
            sync.wait_ge(out_stored, 16 * TB)

        @block.gpsimd
        def _(pool):
            nc.gpsimd.memset(ident[:, :], 0.0).then_inc(const_step, 1)
            nc.gpsimd.memset(power[:, :], -0.5).then_inc(power_ready, 1)
            pool.wait_ge(const_step, 1)
            nc.gpsimd.affine_select(out=ident[:, :], in_=ident[:, :], compare_op=ALU.not_equal, fill=1.0, base=0,
                                    pattern=[[-1, P]], channel_multiplier=1).then_inc(ident_ready, 1)

            def rstd_of(n, b):
                pool.wait_ge(vareps_ready, TB * n + b + 1)
                nc.gpsimd.tensor_tensor(rstd[:, b:b + 1], vareps[:, b:b + 1], power[:, :],
                                        ALU.pow).then_inc(rstd_ready, 1)

            pool.wait_ge(power_ready, 1)
            for b in range(TB):
                rstd_of(0, b)
            nc.gpsimd.memset(headmask[:, :], 1.0).then_inc(const_step, 1)
            nc.gpsimd.memset(ones_row[:, :], 1.0).then_inc(consts_ready, 1)
            nc.gpsimd.iota(slot_no[:, :], pattern=[[1, CAP]], base=1, channel_multiplier=0,
                           allow_small_or_imprecise_dtypes=True).then_inc(consts_ready, 1)
            pool.wait_ge(const_step, 2)
            nc.gpsimd.affine_select(out=headmask[:, :], in_=headmask[:, :], compare_op=ALU.is_ge, fill=0.0, base=0,
                                    pattern=[[-HD, HPT]], channel_multiplier=1).then_inc(const_step, 1)
            pool.wait_ge(const_step, 3)
            nc.gpsimd.affine_select(out=headmask[:, :], in_=headmask[:, :], compare_op=ALU.is_ge, fill=0.0,
                                    base=HD - 1, pattern=[[HD, HPT]],
                                    channel_multiplier=-1).then_inc(consts_ready, 1)

            pool.wait_ge(scores_ready, 2 * 6)
            for b, at, keys in ((1, 0, 2 * P), (0, 2 * P, P)):
                nc.gpsimd.iota(bias[:, :, at:at + keys], pattern=[[0, NH], [1, keys]], base=-P * b,
                               channel_multiplier=-1, allow_small_or_imprecise_dtypes=True).then_inc(bias_step, 1)
            pool.wait_ge(bias_step, 2)
            for h in range(NH):
                nc.gpsimd.tensor_scalar(bias[:, h], bias[:, h], SLOPES[h], None, ALU.mult).then_inc(bias_step, 1)
            for h in range(NH):
                if h == 0:
                    pool.wait_ge(bias_step, 2 + NH)
                for b, at, keys in ((1, 0, 2 * P), (0, 2 * P, P)):
                    nc.gpsimd.affine_select(out=bias[:, h, at:at + keys], in_=bias[:, h, at:at + keys],
                                            compare_op=ALU.is_ge, fill=MASKED, base=P * b, pattern=[[-1, keys]],
                                            channel_multiplier=1).then_inc(bias_ready, 1)
            pool.wait_ge(chunk_out_ready, 2 * 6)
            nc.gpsimd.memset(vaug[:, :, :, HD:2 * HD], 1.0).then_inc(vones_ready, 1)
            for b in range(TB):
                rstd_of(1, b)
            pool.wait_ge(k_plain_ready, 1)
            pool.wait_ge(consts_ready, 3)
            for h in range(4, NH):
                nc.gpsimd.tensor_scalar(kM[:, h], k_plain[:, h // HPT], headmask[:, h % HPT:h % HPT + 1], None,
                                        ALU.mult).then_inc(kM_ready, 1)
            for b in range(TB):
                rstd_of(2, b)
            pool.wait_ge(onehot_ready, 1)
            nc.gpsimd.tensor_tensor(weighted[:, :, :].rearrange("p b (e j) -> p (b e) j", j=CAP),
                                    onehot[:, :, :].rearrange("p b (e j) -> p (b e) j", j=CAP),
                                    pw[:, 1].rearrange("p b e -> p (b e)").unsqueeze(2).to_broadcast([P, TB * E, CAP]),
                                    ALU.mult).then_inc(weighted_ready, 1)

        @block.vector
        def _(dve):
            steps = [0]

            def step(ins):
                steps[0] += 1
                ins.then_inc(dve_step, 1)
                dve.wait_ge(dve_step, steps[0])

            def norm_stats(b):
                step(nc.vector.bn_stats(stats[:, b], x_sb[:, b]))
                step(nc.vector.bn_aggr(meanvar[:, b], stats[:, b]))
                nc.vector.tensor_scalar(vareps[:, b:b + 1], meanvar[:, b, 1:2], EPS, None,
                                        ALU.add).then_inc(vareps_ready, 1)

            def norm_apply(n, b):
                dve.wait_ge(rstd_ready, TB * n + b + 1)
                nc.vector.tensor_scalar(xn[:, b], x_sb[:, b], meanvar[:, b, 0:1], rstd[:, b:b + 1], ALU.subtract,
                                        ALU.mult).then_inc(xn_ready, 1)

            dve.wait_ge(x_loaded, 16)
            for b in range(TB):
                norm_stats(b)
            for b in range(TB):
                norm_apply(0, b)

            def first_max(b):
                dve.wait_ge(scores_ready, b + 1)
                nc.vector.tensor_reduce(negmax[:, b, 0:1], s_bank[b][:, :], AX.X, ALU.max,
                                        negate=True).then_inc(negmax_ready, 1)

            def next_max(i, b):
                dve.wait_ge(scores_ready, i * 2 + (b + 1))
                nc.vector.tensor_reduce(chunkneg[:, b:b + 1], s_bank[b][:, :], AX.X, ALU.max,
                                        negate=True).then_inc(chunkmax_ready, 1)
                dve.wait_ge(chunkmax_ready, i * 2 + (b - 1))
                nc.vector.tensor_tensor(negmax[:, b, bass.ds(i, 1)], chunkneg[:, b:b + 1],
                                        negmax[:, b, bass.ds(i - 1, 1)], ALU.min).then_inc(negmax_ready, 1)

            def first_out(b):
                dve.wait_ge(probs_ready, b + 1)
                nc.vector.tensor_copy(denom[:, b:b + 1], rowsum[:, b, 0:1]).then_inc(denom_ready, 1)
                dve.wait_ge(chunk_out_ready, b + 1)
                nc.vector.tensor_copy(acc[:, b], o_bank[b][:, 0:C]).then_inc(acc_ready, 1)

            def next_out(i, b):
                dve.wait_ge(shrink_ready, i * 2 + (b - 1))
                dve.wait_ge(probs_ready, i * 2 + (b + 1))
                dve.wait_ge(denom_ready, i * 2 + (b - 1))
                nc.vector.scalar_tensor_tensor(denom[:, b:b + 1], denom[:, b:b + 1], shrink[:, b, bass.ds(i, 1)],
                                               rowsum[:, b, bass.ds(i, 1)], ALU.mult,
                                               ALU.add).then_inc(denom_ready, 1)
                dve.wait_ge(chunk_out_ready, i * 2 + (b + 1))
                dve.wait_ge(acc_ready, i * 2 + (b - 1))
                nc.vector.scalar_tensor_tensor(acc[:, b], acc[:, b], shrink[:, b, bass.ds(i, 1)],
                                               o_bank[b][:, 0:C], ALU.mult, ALU.add).then_inc(acc_ready, 1)

            for b in range(TB):
                first_max(b)
            for b in range(TB):
                next_max(1, b)
                first_out(b)
            with dve.Fori(1, NCH - 1) as i:
                for b in range(TB):
                    next_max(i + 1, b)
                    next_out(i, b)
            for b in range(TB):
                next_out(NCH - 1, b)
                dve.wait_ge(denom_ready, TB * (NCH - 1) + b + 1)
                dve.wait_ge(acc_ready, TB * (NCH - 1) + b + 1)
                step(nc.vector.reciprocal(rdenom[:, b:b + 1], denom[:, b:b + 1]))
                step(nc.vector.scalar_tensor_tensor(x_sb[:, b], acc[:, b], rdenom[:, b:b + 1], x_sb[:, b], ALU.mult,
                                                    ALU.add))
                norm_stats(b)
                norm_apply(1, b)

            dve.wait_ge(k_plain_ready, 1)
            dve.wait_ge(consts_ready, 3)
            nc.vector.tensor_tensor(kM[:, 0:4], k_plain[:, 0].unsqueeze(1).to_broadcast([P, 4, T]),
                                    headmask[:, 0:4].unsqueeze(2).to_broadcast([P, 4, T]),
                                    ALU.mult).then_inc(kM0_ready, 1)

            def bias_unit(n):
                g, b, heads, keys = units(n)
                dve.wait_ge(ascores_ready, n + 1)
                if n == 0:
                    dve.wait_ge(bias_ready, 2 * NH)
                if n >= 3:
                    dve.wait_ge(aprobs_ready, n - 2)
                for m, j in enumerate(heads):
                    at = (1 - b) * 2 * P
                    last = nc.vector.tensor_tensor_reduce(
                        out=biased[:, n % 3, m * keys:(m + 1) * keys], in0=as_bank[n % 3][:, m * keys:(m + 1) * keys],
                        in1=bias[:, 4 * g + j, at:at + keys], scale=-1.0, scalar=-MASKED, op0=ALU.add, op1=ALU.min,
                        accum_out=nmax[:, n, m:m + 1])
                last.then_inc(biased_ready, 1)

            def copy_q0(g):
                n = 3 * g
                dve.wait_ge(aprobsT_in_psum, n + 1)
                if g >= 2:
                    dve.wait_ge(y_in_psum, g - 1)
                nc.vector.tensor_copy(aprobsT[:, g % 2, :, 0], at_bank[n % 2][:, :].rearrange(
                    "p (h q) -> p h q", h=4)).then_inc(aprobsT_q0_ready, 1)

            def normalize_y(g):
                dve.wait_ge(y_in_psum, g + 1)
                step(nc.vector.stream_shuffle(r_T[:, :], y_ps, [HD + m % HD for m in range(32)]))
                step(nc.vector.reciprocal(r_T[:, :], r_T[:, :]))
                nc.vector.tensor_tensor(y_T[:, g], y_ps, r_T[:, :], ALU.mult).then_inc(y_T_ready, 1)
                dve.wait_ge(y_T_ready, g + 1)

            for n in range(NU + 4):
                if n < NU:
                    bias_unit(n)
                if n >= 2 and (n - 2) % 3 == 0 and (n - 2) // 3 < NG:
                    copy_q0((n - 2) // 3)
                if n >= 6 and (n - 6) % 3 == 0:
                    normalize_y((n - 6) // 3)

            for b in range(TB):
                dve.wait_ge(proj_ready, b + 1)
                step(nc.vector.tensor_tensor(x_sb[:, b], proj_ps[b], x_sb[:, b], ALU.add))
                norm_stats(b)
                norm_apply(2, b)

            dve.wait_ge(router_in_psum, 1)
            nc.vector.tensor_copy(scores[:, :], router_ps)
            step(nc.vector.tensor_copy(work[:, :], router_ps))
            for r in range(CAP // 8):
                best = top[:, 8 * r:8 * r + 8]
                step(nc.vector.max(best, work[:, :]))
                if r == 0:
                    nc.vector.tensor_scalar(negtop[:, :], top[:, 0:1], -1.0, None, ALU.mult).then_inc(negtop_ready, 1)
                step(nc.vector.match_replace(out=work[:, :], in_to_replace=best, in_values=work[:, :],
                                             imm_value=TAKEN))
            step(nc.vector.tensor_scalar(taken[:, :], work[:, :], TAKEN / 2, None, ALU.is_le))
            step(nc.vector.tensor_tensor_scan(place[:, 0], ones_row[:, :], taken[:, :], 0.0, ALU.mult, ALU.add))
            nc.vector.tensor_tensor(place[:, 0], place[:, 0], taken[:, :], ALU.mult).then_inc(place_ready, 1)
            dve.wait_ge(expd_ready, 1)
            step(nc.vector.tensor_tensor_reduce(out=expd[:, :], in0=expd[:, :], in1=taken[:, :], scale=1.0,
                                                scalar=0.0, op0=ALU.mult, op1=ALU.add, accum_out=wsum[:, :]))
            step(nc.vector.reciprocal(wsum[:, :], wsum[:, :]))
            nc.vector.tensor_scalar(place[:, 1], expd[:, :], wsum[:, :], None, ALU.mult).then_inc(weight_ready, 1)
            dve.wait_ge(pw_in_psum, 1)
            step(nc.vector.tensor_copy(pw[:, :, :, :].rearrange("p a b e -> p (a b e)"), pw_ps))
            nc.vector.tensor_tensor(onehot[:, :, :].rearrange("p b (e j) -> p (b e) j", j=CAP),
                                    pw[:, 0].rearrange("p b e -> p (b e)").unsqueeze(2).to_broadcast([P, TB * E, CAP]),
                                    slot_no[:, :].unsqueeze(1).to_broadcast([P, TB * E, CAP]),
                                    ALU.is_equal).then_inc(onehot_ready, 1)
            dve.wait_ge(xg_in_psum, 2)
            nc.vector.tensor_copy(xg_T[:, 1], xg_ps[1]).then_inc(xg1_ready, 1)
            for g in range(EG):
                dve.wait_ge(silu_ready, g + 1)
                dve.wait_ge(up_in_psum, g + 1)
                nc.vector.tensor_tensor(act[:, g], up_ps[g][1][:, :], act[:, g], ALU.mult).then_inc(act_ready, 1)
            for g in range(EG):
                dve.wait_ge(down_in_psum, g + 1)
                nc.vector.tensor_copy(y_e[:, g], down_ps[g]).then_inc(y_e_ready, 1)
            for b in range(TB):
                dve.wait_ge(moe_in_psum, b + 1)
                nc.vector.tensor_tensor(x_out[:, b], moe_ps[b], x_sb[:, b], ALU.add).then_inc(x_final, 1)

        @block.scalar
        def _(act_eng):
            act_e = act_eng

            def norm_T(n):
                for b in range(TB):
                    act_e.wait_ge(xnT_in_psum, TB * n + b + 1)
                    nc.scalar.activation(xnT[:, :, b * P:(b + 1) * P], ln_ps[b],
                                         ACT.Copy).then_inc(xnT_ready, 1)

            norm_T(0)

            def exps(i, b, first):
                act_e.wait_ge(negmax_ready, i * 2 + (b + 1))
                if not first:
                    act_e.wait_ge(probsT_in_psum, i * 2 + (b - 1))
                nc.scalar.activation(probs[:, b], s_bank[b][:, :], ACT.Exp, bias=negmax[:, b, bass.ds(i, 1)],
                                     accum_out=rowsum[:, b, bass.ds(i, 1)]).then_inc(probs_ready, 1)
                if not first:
                    nc.scalar.activation(shrink[:, b, bass.ds(i, 1)], negmax[:, b, bass.ds(i - 1, 1)], ACT.Exp,
                                         bias=negmax[:, b, bass.ds(i, 1)], scale=-1.0).then_inc(shrink_ready, 1)

            def copy_T(i, b, first=False):
                act_e.wait_ge(probsT_in_psum, i * 2 + (b + 1))
                if not first:
                    act_e.wait_ge(chunk_out_ready, i * 2 + (b - 1))
                nc.scalar.activation(probsT[:, b].rearrange("p n q -> p (n q)"), t_bank[b][:, :],
                                     ACT.Copy).then_inc(probsT_ready, 1)

            for b in range(TB):
                exps(0, b, True)
            for b in range(TB):
                copy_T(0, b, True)
                exps(1, b, False)
            with act_e.Fori(1, NCH - 1) as i:
                for b in range(TB):
                    copy_T(i, b)
                    exps(i + 1, b, False)
            for b in range(TB):
                copy_T(NCH - 1, b)

            norm_T(1)
            act_e.wait_ge(qkv_in_psum, 1)
            nc.scalar.activation(q_T[:, :, :], q_ps, ACT.Copy, scale=HD ** -0.5).then_inc(q_ready, 1)
            act_e.wait_ge(qkv_in_psum, 2)
            nc.scalar.activation(k_plain, k_ps, ACT.Copy).then_inc(k_plain_ready, 1)
            act_e.wait_ge(qkv_in_psum, 3)
            act_e.wait_ge(vones_ready, 1)
            for kb in range(TB):
                last = nc.scalar.activation(vaug[:, kb, :, 0:HD], v_ps[:, kb].rearrange("p (h d) -> p h d", h=NH),
                                            ACT.Copy)
            last.then_inc(vaug_ready, 1)

            def exp_unit(n):
                g, b, heads, keys = units(n)
                act_e.wait_ge(biased_ready, n + 1)
                if n >= 3:
                    act_e.wait_ge(aprobsT_in_psum, n - 2)
                for m in range(len(heads)):
                    last = nc.scalar.activation(aprobs[:, n % 3, m * keys:(m + 1) * keys],
                                                biased[:, n % 3, m * keys:(m + 1) * keys], ACT.Exp,
                                                bias=nmax[:, n, m:m + 1], scale=-1.0)
                last.then_inc(aprobs_ready, 1)

            def copy_q1(n):
                g, b, heads, keys = units(n)
                act_e.wait_ge(aprobsT_in_psum, n + 1)
                if g >= 2:
                    act_e.wait_ge(y_in_psum, g - 1)
                nc.scalar.activation(aprobsT[:, g % 2, heads[0]:heads[0] + 2, 1:3],
                                     at_bank[n % 2][:, :].rearrange("p (h m q) -> p h m q", h=2, m=2),
                                     ACT.Copy).then_inc(aprobsT_q1_ready, 1)

            for n in range(NU + 2):
                if n < NU:
                    exp_unit(n)
                if n >= 2 and (n - 2) % 3:
                    copy_q1(n - 2)

            norm_T(2)
            act_e.wait_ge(negtop_ready, 1)
            nc.scalar.activation(expd[:, :], scores[:, :], ACT.Exp, bias=negtop[:, :]).then_inc(expd_ready, 1)
            act_e.wait_ge(xg_in_psum, 1)
            nc.scalar.activation(xg_T[:, 0], xg_ps[0], ACT.Copy).then_inc(xg0_ready, 1)
            act_e.wait_ge(scatter_in_psum, 1)
            nc.scalar.activation(scatter[:, :, :, :], scatter_ps, ACT.Copy).then_inc(scatter_ready, 1)
            for g in range(EG):
                act_e.wait_ge(gate_in_psum, g + 1)
                nc.scalar.activation(act[:, g], up_ps[g][0][:, :], ACT.Silu).then_inc(silu_ready, 1)
            for g in range(EG):
                act_e.wait_ge(hT_in_psum, g + 1)
                nc.scalar.activation(h_T[:, g].rearrange("p k n -> p (k n)"), hT_ps[g][:, :],
                                     ACT.Copy).then_inc(hT_ready, 1)

        @block.tensor
        def _(pe):
            def norm_T(n):
                for b in range(TB):
                    pe.wait_ge(xn_ready, TB * n + b + 1)
                    for k in range(KC):
                        last = nc.tensor.transpose(ln_ps[b][:, k], xn[:, b, k * P:(k + 1) * P], ident[:, :])
                    last.then_inc(xnT_in_psum, 1)

            pe.wait_ge(ident_ready, 1)
            norm_T(0)

            def scores_of(i, b):
                pe.wait_ge(kT_loaded, i * 16 + 16)
                for k in range(KC):
                    last = nc.tensor.matmul(s_bank[b][:, :], xnT[:, k, b * P:(b + 1) * P], kT[:, i, k],
                                            start=(k == 0), stop=(k == KC - 1))
                last.then_inc(scores_ready, 1)

            def transpose_of(i, b, first=False):
                pe.wait_ge(probs_ready, i * 2 + (b + 1))
                if not first:
                    pe.wait_ge(probsT_ready, i * 2 + (b - 1))
                for n in range(NT):
                    last = nc.tensor.transpose(t_bank[b][:, n * P:(n + 1) * P], probs[:, b, n * P:(n + 1) * P],
                                               ident[:, :])
                last.then_inc(probsT_in_psum, 1)

            def values_of(i, b, first=False):
                pe.wait_ge(probsT_ready, i * 2 + (b + 1))
                pe.wait_ge(v_loaded, i * 16 + 16)
                if not first:
                    pe.wait_ge(acc_ready, i * 2 + (b - 1))
                for n in range(NT):
                    last = nc.tensor.matmul(o_bank[b][:, 0:C], probsT[:, b, n], v_sb[:, i, n], start=(n == 0),
                                            stop=(n == NT - 1))
                last.then_inc(chunk_out_ready, 1)

            for b in range(TB):
                pe.wait_ge(xnT_ready, b + 1)
                scores_of(0, b)
            for b in range(TB):
                transpose_of(0, b, True)
                scores_of(1, b)
                values_of(0, b, True)
            with pe.Fori(1, NCH - 1) as i:
                for b in range(TB):
                    transpose_of(i, b)
                    scores_of(i + 1, b)
                    values_of(i, b)
            for b in range(TB):
                transpose_of(NCH - 1, b)
            for b in range(TB):
                values_of(NCH - 1, b)

            norm_T(1)
            pe.wait_ge(wqkv_loaded, 16)
            pe.wait_ge(xnT_ready, 2 * TB)
            pe.wait_ge(probsT_ready, TB * NCH)
            for which, ps in ((0, q_ps), (1, k_ps)):
                for m in range(2):
                    for k in range(KC):
                        at = which * C + m * P
                        last = nc.tensor.matmul(ps[:, m], wqkv_sb[:, k, at:at + P], xnT[:, k, :],
                                                start=(k == 0), stop=(k == KC - 1))
                last.then_inc(qkv_in_psum, 1)
            for kb in range(TB):
                for k in range(KC):
                    last = nc.tensor.matmul(v_ps[:, kb], xnT[:, k, kb * P:(kb + 1) * P], wqkv_sb[:, k, 2 * C:3 * C],
                                            start=(k == 0), stop=(k == KC - 1))
            last.then_inc(qkv_in_psum, 1)

            def scores_unit(n):
                g, b, heads, keys = units(n)
                if n == 0:
                    pe.wait_ge(q_ready, 1)
                    pe.wait_ge(kM0_ready, 1)
                    pe.wait_ge(acc_ready, TB * NCH)
                if n % 3 == 0 and g:
                    pe.wait_ge(kM_ready, 4 * g)
                if n >= 3:
                    pe.wait_ge(biased_ready, n - 2)
                h = 4 * g + heads[0]
                nc.tensor.matmul(as_bank[n % 3][:, :], q_T[:, h // HPT, b * P:(b + 1) * P],
                                 kM[:, h:h + len(heads), 0:keys], start=True, stop=True).then_inc(ascores_ready, 1)

            def transpose_unit(n):
                pe.wait_ge(aprobs_ready, n + 1)
                if n >= 2:
                    if (n - 2) % 3 == 0:
                        pe.wait_ge(aprobsT_q0_ready, (n - 2) // 3 + 1)
                    else:
                        pe.wait_ge(aprobsT_q1_ready, 2 * ((n - 2) // 3) + (n - 2) % 3)
                for m in range(4):
                    last = nc.tensor.transpose(at_bank[n % 2][:, m * P:(m + 1) * P],
                                               aprobs[:, n % 3, m * P:(m + 1) * P], ident[:, :])
                last.then_inc(aprobsT_in_psum, 1)

            def values_group(g):
                pe.wait_ge(aprobsT_q0_ready, g + 1)
                pe.wait_ge(aprobsT_q1_ready, 2 * g + 2)
                if g == 0:
                    pe.wait_ge(vaug_ready, 1)
                    pe.wait_ge(k_plain_ready, 1)
                else:
                    pe.wait_ge(y_T_ready, g)
                for j in range(4):
                    nc.tensor.matmul(y_ps[32 * j:32 * j + 32, :], vaug[:, 0, 4 * g + j],
                                     aprobsT[:, g % 2, j, 0:2].rearrange("p m q -> p (m q)"), start=True, stop=False)
                for j in range(4):
                    last = nc.tensor.matmul(y_ps[32 * j:32 * j + 32, P:2 * P], vaug[:, 1, 4 * g + j],
                                            aprobsT[:, g % 2, j, 2], start=False, stop=True)
                last.then_inc(y_in_psum, 1)

            def project(g):
                pe.wait_ge(y_T_ready, g + 1)
                if g == 0:
                    pe.wait_ge(wproj_loaded, 16)
                for b in range(TB):
                    last = nc.tensor.matmul(proj_ps[b], y_T[:, g, b * P:(b + 1) * P], wproj_sb[:, g],
                                            start=(g == 0), stop=(g == NG - 1))
                    if g == NG - 1:
                        last.then_inc(proj_ready, 1)

            scores_unit(0)
            scores_unit(1)
            for n in range(NU + 4):
                if n + 2 < NU:
                    scores_unit(n + 2)
                if n < NU:
                    transpose_unit(n)
                if n >= 3 and n % 3 == 0 and n // 3 - 1 < NG:
                    values_group(n // 3 - 1)
                if n >= 5 and (n - 5) % 3 == 0:
                    project((n - 5) // 3)

            norm_T(2)
            pe.wait_ge(wg_loaded, 16)
            pe.wait_ge(xnT_ready, 3 * TB)
            for k in range(KC):
                last = nc.tensor.matmul(router_ps, wg_sb[:, k], xnT[:, k], start=(k == 0), stop=(k == KC - 1))
            last.then_inc(router_in_psum, 1)
            for a, ready in ((0, place_ready), (1, weight_ready)):
                pe.wait_ge(ready, 1)
                for b in range(TB):
                    at = (a * TB + b) * E
                    last = nc.tensor.transpose(pw_ps[:, at:at + E], place[:, a, b * P:(b + 1) * P], ident[0:E, 0:E])
            last.then_inc(pw_in_psum, 1)
            pe.wait_ge(onehot_ready, 1)
            for k in range(KC):
                for b in range(TB):
                    last = nc.tensor.matmul(xg_ps[k], xn[:, b, k * P:(k + 1) * P], onehot[:, b],
                                            start=(b == 0), stop=(b == TB - 1))
                last.then_inc(xg_in_psum, 1)
            pe.wait_ge(weighted_ready, 1)
            for g in range(EG):
                for b in range(TB):
                    last = nc.tensor.transpose(scatter_ps[:, g, b], weighted[:, b, g * P:(g + 1) * P], ident[:, :])
            last.then_inc(scatter_in_psum, 1)
            pe.wait_ge(xg0_ready, 1)
            pe.wait_ge(xg1_ready, 1)
            for g in range(EG):
                pe.wait_ge(wup_loaded[g], 16)
                for w, ready in ((0, gate_in_psum), (1, up_in_psum)):
                    for k in range(KC):
                        for j in range(4):
                            e = 4 * g + j
                            last = nc.tensor.matmul(up_ps[g][w][32 * j:32 * j + 32, :],
                                                    xg_T[:, k, e * CAP:(e + 1) * CAP], wup_sb[:, e, w, k],
                                                    start=(k == 0), stop=(k == KC - 1))
                    last.then_inc(ready, 1)
            for g in range(EG):
                pe.wait_ge(act_ready, g + 1)
                if g == 1:
                    pe.wait_ge(scatter_ready, 1)
                for k in range(KH):
                    last = nc.tensor.transpose(hT_ps[g][:, k * P:(k + 1) * P], act[:, g, k * P:(k + 1) * P],
                                               ident[:, :])
                last.then_inc(hT_in_psum, 1)
            for g in range(EG):
                pe.wait_ge(hT_ready, g + 1)
                pe.wait_ge(wdn_loaded[g], 16)
                for k in range(KH):
                    for j in range(4):
                        last = nc.tensor.matmul(down_ps[g][32 * j:32 * j + 32, :], h_T[:, g, k, 32 * j:32 * j + 32],
                                                wdn_sb[:, 4 * g + j, k], start=(k == 0), stop=(k == KH - 1))
                last.then_inc(down_in_psum, 1)
            pe.wait_ge(scatter_ready, 1)
            for b in range(TB):
                for g in range(EG):
                    pe.wait_ge(y_e_ready, g + 1)
                    last = nc.tensor.matmul(moe_ps[b], scatter[:, g, b], y_e[:, g], start=(g == 0),
                                            stop=(g == EG - 1))
                last.then_inc(moe_in_psum, 1)


def kernel(x, ctx_1024, L0_attn_w_attn, L0_attn_w_proj, L0_ffn_Wg, L0_ffn_W1, L0_ffn_W2, L0_ffn_W3):
    import numpy as np
    import concourse.bacc as bacc
    from concourse.bass_utils import run_bass_kernel_spmd

    def rows(a, n):
        return a.reshape(n, P, -1).transpose(1, 0, 2)

    ctx = np.asarray(ctx_1024)[0]
    w_proj = np.asarray(L0_attn_w_proj)
    padded = np.zeros((P, NG, C), w_proj.dtype)
    padded.reshape(4, 32, NG, C)[:, 0:HD] = w_proj.T.reshape(NG, 4, HD, C).transpose(1, 2, 0, 3)
    up = [np.asarray(w).transpose(2, 0, 1).reshape(KC, P, E, H).transpose(1, 2, 0, 3)
          for w in (L0_ffn_W1, L0_ffn_W3)]
    arrays = {
        "x_in": rows(np.asarray(x)[0], TB),
        "ctx_t": ctx.reshape(NCH, CH, KC, P).transpose(0, 3, 2, 1),
        "ctx_v": ctx.reshape(NCH, NT, P, C).transpose(0, 2, 1, 3),
        "w_qkv": rows(np.asarray(L0_attn_w_attn).T, KC),
        "w_proj": padded,
        "w_gate": rows(np.asarray(L0_ffn_Wg).T, KC),
        "w_up": np.stack(up, axis=2),
        "w_down": np.asarray(L0_ffn_W2).transpose(2, 0, 1).reshape(KH, P, E, C).transpose(1, 2, 0, 3),
    }
    arrays = {k: np.ascontiguousarray(a) for k, a in arrays.items()}
    nc = bacc.Bacc("TRN2", target_bir_lowering=False, num_devices=1)
    aps = [nc.dram_tensor(k, a.shape, mybir.dt.from_np(a.dtype), kind="ExternalInput").ap()
           for k, a in arrays.items()]
    aps.append(nc.dram_tensor("x_out_dram", (P, TB, C), FP32, kind="ExternalOutput").ap())
    build(nc, *aps)
    r = run_bass_kernel_spmd(nc, [arrays], core_ids=[0])
    return r.results[0]["x_out_dram"].transpose(1, 0, 2).reshape(1, T, C)
```

```python
from contextlib import ExitStack

import concourse.bass as bass
import concourse.mybir as mybir

FP32 = mybir.dt.float32
FP32R = mybir.dt.float32r
ALU = mybir.AluOpType
ACT = mybir.ActivationFunctionType
AX = mybir.AxisListType

P = 128
T, C, S = 256, 256, 4096
TB, KC = T // P, C // P
CH = 512
NCH = S // CH
NT = CH // P
NH, HD = 16, 16
NG = NH // 4
HPT = P // HD
E, H, CAP = 8, 512, 32
KH = H // P
EG = E // 4
EPS = 1e-5
MASKED = -1e30
TAKEN = -3e38
SLOPES = [2.0 ** (-0.5 * (h + 1)) for h in range(NH)]


def units(n):
    g, kind = n // 3, n % 3
    return (g, 0, range(0, 4), P) if kind == 0 else (g, 1, range(2 * kind - 2, 2 * kind), 2 * P)


NU = 3 * NG


def build(nc, x, ctx_t, ctx_v, w_qkv, w_proj, w_gate, w_up, w_down, out):
    es = ExitStack()
    with es:
        def sb(name, shape, dtype=FP32):
            return es.enter_context(nc.sbuf_tensor(name, shape, dtype))

        def carve(region, size, pattern, **axes):
            part = region[0][:, region[1]:region[1] + size]
            region[1] += size
            return part.rearrange(pattern, **axes)

        def sem(name):
            return es.enter_context(nc.semaphore(name))

        x_sb = sb("x_sb", [P, TB, C])
        v_sb = sb("v_sb", [P, NCH, NT, C])
        wqkv_sb = sb("wqkv_sb", [P, KC, 3 * C])
        wproj_sb = sb("wproj_sb", [P, NG, C])
        wg_sb = sb("wg_sb", [P, KC, E])
        wup_sb = sb("wup_sb", [P, E, 2, KC, H])
        wdn_sb = sb("wdn_sb", [P, E, KH, C])
        kT = wdn_sb[:, :, :, :].rearrange("p e k c -> p (e k c)").rearrange("p (i k s) -> p i k s", i=NCH, k=KC)
        ident = sb("ident", [P, P])
        power = sb("power", [P, 1])
        headmask = sb("headmask", [P, HPT])
        slot_no = sb("slot_no", [P, CAP])
        ones_row = sb("ones_row", [E, T])
        stats = sb("stats", [P, TB, 6])
        meanvar = sb("meanvar", [P, TB, 2])
        vareps = sb("vareps", [P, TB])
        rstd = sb("rstd", [P, TB])
        xn = sb("xn", [P, TB, C])
        xnT = sb("xnT", [P, KC, T])
        negmax = sb("negmax", [P, TB, NCH])
        chunkneg = sb("chunkneg", [P, TB])
        shrink = sb("shrink", [P, TB, NCH])
        rowsum = sb("rowsum", [P, TB, NCH])
        denom = sb("denom", [P, TB])
        rdenom = sb("rdenom", [P, TB])
        acc = sb("acc", [P, TB, C])
        q_hi = sb("q_hi", [P, KC, T], FP32R)
        q_lo = sb("q_lo", [P, KC, T], FP32R)
        k_hi = sb("k_hi", [P, 2, KC, CH], FP32R)
        k_lo = sb("k_lo", [P, 2, KC, CH], FP32R)
        v_hi = sb("v_hi", [P, 2, NT, C], FP32R)
        v_lo = sb("v_lo", [P, 2, NT, C], FP32R)
        p_hi = sb("p_hi", [P, TB, NT, P], FP32R)
        p_lo = sb("p_lo", [P, TB, NT, P], FP32R)
        before_up = [wup_sb[:, 4:8].rearrange("p e w k h -> p (e w k h)"), 0]
        before_dn = [wdn_sb[:, 4:8].rearrange("p e k c -> p (e k c)"), 0]
        over_v = [v_sb[:, :, :, :].rearrange("p i n c -> p (i n c)"), 0]
        bias = carve(before_up, NH * 3 * P, "p (h k) -> p h k", h=NH)
        probs = before_up[0][:, before_up[1]:before_up[1] + TB * CH].rearrange("p (b k) -> p b k", b=TB)
        biased = carve(before_up, 3 * 512, "p (s k) -> p s k", s=3)
        aprobsT = carve(before_dn, 2 * 4 * 3 * P, "p (s h m q) -> p s h m q", s=2, h=4, m=3)
        y_T = carve(before_dn, NG * T, "p (g t) -> p g t", g=NG)
        kM = carve(over_v, NH * T, "p (h k) -> p h k", h=NH)
        k_plain = carve(over_v, 2 * T, "p (m t) -> p m t", m=2)
        vpad = carve(over_v, TB * NH * 32, "p (k h d) -> p k h d", k=TB, h=NH)
        aprobs = carve(over_v, 3 * 512, "p (s k) -> p s k", s=3)
        q_T = carve(over_v, 2 * T, "p (m t) -> p m t", m=2)
        nmax = sb("nmax", [P, NU, 4])
        asum = sb("asum", [P, NG, TB, 4])
        rsum = sb("rsum", [P, TB, 4])
        rwide = sb("rwide", [P, TB, 4, 32])
        r_T = sb("r_T", [P, T])
        rel = sb("rel", [P, 3 * P])

        scores = sb("scores", [E, T])
        work = sb("work", [E, T])
        top = sb("top", [E, CAP])
        negtop = sb("negtop", [E, 1])
        expd = sb("expd", [E, T])
        taken = sb("taken", [E, T])
        place = sb("place", [E, 2, T])
        wsum = sb("wsum", [E, 1])
        pw = sb("pw", [P, TB * E])
        over_v[1] = 0
        onehot = carve(over_v, TB * E * CAP, "p (b n) -> p b n", b=TB)
        weighted = carve(over_v, TB * E * CAP, "p (b n) -> p b n", b=TB)
        scatter = carve(over_v, EG * TB * P, "p (g b t) -> p g b t", g=EG, b=TB)
        xg_T = carve(over_v, KC * E * CAP, "p (k n) -> p k n", k=KC)
        act = carve(over_v, EG * H, "p (g h) -> p g h", g=EG)
        h_T = carve(over_v, EG * KH * P, "p (g k n) -> p g k n", g=EG, k=KH)
        y_e = carve(over_v, EG * C, "p (g c) -> p g c", g=EG)
        x_out = carve(over_v, TB * C, "p (b c) -> p b c", b=TB)

        banks = [es.enter_context(nc.psum_tensor(f"bank{i}", [P, 512], FP32)) for i in range(8)]
        s_bank, t_bank, o_bank = banks[0:2], banks[4:6], banks[6:8]
        ln_ps = [banks[2 + b][:, 0:C].rearrange("p (k t) -> p k t", k=KC) for b in range(TB)]
        k_ps, q_ps = ([banks[i][:, 0:C].rearrange("p (m t) -> p m t", m=2) for i in pair] for pair in ((1, 6), (0, 5)))
        v_ps = [banks[i][:, 0:C] for i in (4, 7)]
        as_bank = [banks[0], banks[1], banks[6]]
        at_bank = [banks[7], banks[2]]
        y_ps = banks[4][:, 0:T]
        r_ps = banks[4][:, T:2 * T]
        proj_ps = [banks[3][:, 0:C], banks[5][:, 0:C]]

        router_ps = banks[0][0:E, 0:T]
        place_ps = [banks[1][:, 0:TB * E], banks[4][:, 0:TB * E]]
        xg_ps = [banks[3][:, 0:E * CAP], banks[2][:, 0:E * CAP]]
        scatter_ps = banks[0][:, :].rearrange("p (g b t) -> p g b t", g=EG, b=TB)
        up_ps = [[banks[4], banks[5]], [banks[6], banks[7]]]
        hT_ps = [banks[1], banks[0]]
        down_ps = [banks[2][:, 0:C], banks[3][:, 0:C]]
        moe_ps = [banks[4][:, 0:C], banks[5][:, 0:C]]

        x_loaded = sem("x_loaded")
        kT_loaded = sem("kT_loaded")
        v_loaded = sem("v_loaded")
        wqkv_loaded = sem("wqkv_loaded")
        wproj_loaded = sem("wproj_loaded")
        wg_loaded = sem("wg_loaded")
        wup_loaded = [sem(f"wup_loaded{g}") for g in range(EG)]
        wdn_loaded = [sem(f"wdn_loaded{g}") for g in range(EG)]
        out_stored = sem("out_stored")
        const_step = sem("const_step")
        ident_ready = sem("ident_ready")
        power_ready = sem("power_ready")
        consts_ready = sem("consts_ready")
        dve_step = sem("dve_step")
        vareps_ready = sem("vareps_ready")
        rstd_ready = sem("rstd_ready")
        xn_ready = sem("xn_ready")
        xnT_in_psum = sem("xnT_in_psum")
        xnT_ready = sem("xnT_ready")
        scores_ready = sem("scores_ready")
        chunkmax_ready = sem("chunkmax_ready")
        negmax_ready = sem("negmax_ready")
        probs_ready = sem("probs_ready")
        shrink_ready = sem("shrink_ready")
        probsT_in_psum = sem("probsT_in_psum")
        q_hi_ready = sem("q_hi_ready")
        q_lo_ready = sem("q_lo_ready")
        k_hi_ready = sem("k_hi_ready")
        k_lo_ready = sem("k_lo_ready")
        v_hi_ready = sem("v_hi_ready")
        v_lo_ready = sem("v_lo_ready")
        p_hi_ready = sem("p_hi_ready")
        p_lo_ready = sem("p_lo_ready")
        chunk_out_ready = sem("chunk_out_ready")
        denom_ready = sem("denom_ready")
        acc_ready = sem("acc_ready")
        qkv_in_psum = sem("qkv_in_psum")
        q_ready = sem("q_ready")
        k_plain_ready = sem("k_plain_ready")
        vpad_ready = sem("vpad_ready")
        rel_step = sem("rel_step")
        rel_ready = sem("rel_ready")
        vzero_ready = sem("vzero_ready")
        kM_ready = [sem(f"kM_ready{g}") for g in range(NG)]
        rwide_ready = sem("rwide_ready")
        ascores_ready = sem("ascores_ready")
        biased_ready = sem("biased_ready")
        aprobs_ready = sem("aprobs_ready")
        aprobsT_in_psum = sem("aprobsT_in_psum")
        aprobsT_q0_ready = sem("aprobsT_q0_ready")
        aprobsT_q1_ready = sem("aprobsT_q1_ready")
        y_in_psum = sem("y_in_psum")
        y_T_ready = sem("y_T_ready")
        proj_ready = sem("proj_ready")

        router_in_psum = sem("router_in_psum")
        negtop_ready = sem("negtop_ready")
        expd_ready = sem("expd_ready")
        place_ready = sem("place_ready")
        weight_ready = sem("weight_ready")
        wsum_ready = sem("wsum_ready")
        place_in_psum = sem("place_in_psum")
        pw_ready = sem("pw_ready")
        onehot_ready = sem("onehot_ready")
        weighted_ready = sem("weighted_ready")
        xg_in_psum = sem("xg_in_psum")
        xg0_ready = sem("xg0_ready")
        xg1_ready = sem("xg1_ready")
        scatter_in_psum = sem("scatter_in_psum")
        scatter_ready = sem("scatter_ready")
        gate_in_psum = sem("gate_in_psum")
        up_in_psum = sem("up_in_psum")
        silu_ready = sem("silu_ready")
        act_ready = sem("act_ready")
        hT_in_psum = sem("hT_in_psum")
        hT_ready = sem("hT_ready")
        down_in_psum = sem("down_in_psum")
        y_e_ready = sem("y_e_ready")
        moe_in_psum = sem("moe_in_psum")
        x_final = sem("x_final")

        block = es.enter_context(nc.Block())

        @block.sync
        def _(sync):
            sync.dma_start(x_sb[:, :, :], x).then_inc(x_loaded, 16)
            sync.dma_start(kT[:, 0], ctx_t[0]).then_inc(kT_loaded, 16)
            sync.dma_start(v_sb[:, 0], ctx_v[0]).then_inc(v_loaded, 16)
            for i in range(1, NCH):
                sync.wait_ge(kT_loaded, i * 16)
                sync.dma_start(kT[:, i], ctx_t[i]).then_inc(kT_loaded, 16)
                sync.wait_ge(v_loaded, i * 16)
                sync.dma_start(v_sb[:, i], ctx_v[i]).then_inc(v_loaded, 16)
            sync.dma_start(wqkv_sb[:, :, :], w_qkv).then_inc(wqkv_loaded, 16)
            sync.dma_start(wproj_sb[:, :, :], w_proj).then_inc(wproj_loaded, 16)
            sync.dma_start(wg_sb[:, :, :], w_gate).then_inc(wg_loaded, 16)
            sync.dma_start(wup_sb[:, 0:4], w_up[:, 0:4]).then_inc(wup_loaded[0], 16)
            sync.wait_ge(k_lo_ready, NCH)
            sync.dma_start(wdn_sb[:, 0:4], w_down[:, 0:4]).then_inc(wdn_loaded[0], 16)
            sync.wait_ge(aprobs_ready, NU)
            sync.dma_start(wup_sb[:, 4:8], w_up[:, 4:8]).then_inc(wup_loaded[1], 16)
            sync.wait_ge(proj_ready, TB)
            sync.dma_start(wdn_sb[:, 4:8], w_down[:, 4:8]).then_inc(wdn_loaded[1], 16)
            for b in range(TB):
                sync.wait_ge(x_final, b + 1)
                sync.dma_start(out[:, b], x_out[:, b]).then_inc(out_stored, 16)
            sync.wait_ge(out_stored, 16 * TB)

        @block.gpsimd
        def _(pool):
            nc.gpsimd.memset(ident[:, :], 0.0).then_inc(const_step, 1)
            nc.gpsimd.memset(power[:, :], -0.5).then_inc(power_ready, 1)
            pool.wait_ge(const_step, 1)
            nc.gpsimd.affine_select(out=ident[:, :], in_=ident[:, :], compare_op=ALU.not_equal, fill=1.0, base=0,
                                    pattern=[[-1, P]], channel_multiplier=1).then_inc(ident_ready, 1)

            def rstd_of(n, b):
                pool.wait_ge(vareps_ready, TB * n + b + 1)
                nc.gpsimd.tensor_tensor(rstd[:, b:b + 1], vareps[:, b:b + 1], power[:, :],
                                        ALU.pow).then_inc(rstd_ready, 1)

            pool.wait_ge(power_ready, 1)
            for b in range(TB):
                rstd_of(0, b)
            nc.gpsimd.iota(rel[:, 0:2 * P], pattern=[[1, 2 * P]], base=-P, channel_multiplier=-1,
                           allow_small_or_imprecise_dtypes=True).then_inc(rel_step, 1)
            nc.gpsimd.iota(rel[:, 2 * P:], pattern=[[1, P]], base=0, channel_multiplier=-1,
                           allow_small_or_imprecise_dtypes=True).then_inc(rel_step, 1)
            pool.wait_ge(rel_step, 2)
            nc.gpsimd.affine_select(out=rel[:, 0:2 * P], in_=rel[:, 0:2 * P], compare_op=ALU.is_ge, fill=MASKED,
                                    base=P, pattern=[[-1, 2 * P]], channel_multiplier=1).then_inc(rel_ready, 1)
            nc.gpsimd.affine_select(out=rel[:, 2 * P:], in_=rel[:, 2 * P:], compare_op=ALU.is_ge, fill=MASKED,
                                    base=0, pattern=[[-1, P]], channel_multiplier=1).then_inc(rel_ready, 1)
            nc.gpsimd.memset(headmask[:, :], 1.0).then_inc(const_step, 1)
            nc.gpsimd.memset(ones_row[:, :], 1.0).then_inc(consts_ready, 1)
            nc.gpsimd.iota(slot_no[:, :], pattern=[[1, CAP]], base=1, channel_multiplier=0,
                           allow_small_or_imprecise_dtypes=True).then_inc(consts_ready, 1)
            pool.wait_ge(const_step, 2)
            nc.gpsimd.affine_select(out=headmask[:, :], in_=headmask[:, :], compare_op=ALU.is_ge, fill=0.0, base=0,
                                    pattern=[[-HD, HPT]], channel_multiplier=1).then_inc(const_step, 1)
            pool.wait_ge(const_step, 3)
            nc.gpsimd.affine_select(out=headmask[:, :], in_=headmask[:, :], compare_op=ALU.is_ge, fill=0.0,
                                    base=HD - 1, pattern=[[HD, HPT]],
                                    channel_multiplier=-1).then_inc(consts_ready, 1)


            def split_lo(i, kind):
                if kind == "k":
                    pool.wait_ge(k_hi_ready, i + 1)
                    nc.gpsimd.tensor_tensor(k_lo[:, i % 2], kT[:, i], k_hi[:, i % 2].bitcast(FP32),
                                            ALU.subtract).then_inc(k_lo_ready, 1)
                else:
                    pool.wait_ge(v_hi_ready, i + 1)
                    nc.gpsimd.tensor_tensor(v_lo[:, i % 2], v_sb[:, i], v_hi[:, i % 2].bitcast(FP32),
                                            ALU.subtract).then_inc(v_lo_ready, 1)

            split_lo(0, "v")
            pool.wait_ge(k_lo_ready, 1)
            split_lo(1, "k")
            split_lo(2, "k")
            split_lo(1, "v")
            with pool.Fori(1, NCH - 2) as i:
                split_lo(i + 2, "k")
                split_lo(i + 1, "v")
            split_lo(NCH - 1, "v")
            pool.wait_ge(v_lo_ready, NCH)
            nc.gpsimd.memset(vpad[:, :, :, HD:2 * HD], 0.0).then_inc(vzero_ready, 1)
            for b in range(TB):
                rstd_of(1, b)
            pool.wait_ge(k_plain_ready, TB)
            pool.wait_ge(consts_ready, 3)
            for g in (1, 3):
                for h in range(4 * g, 4 * g + 4):
                    nc.gpsimd.tensor_scalar(kM[:, h], k_plain[:, h // HPT], headmask[:, h % HPT:h % HPT + 1], None,
                                            ALU.mult).then_inc(kM_ready[g], 1)
            for b in range(TB):
                rstd_of(2, b)
            pool.wait_ge(onehot_ready, 1)
            pool.wait_ge(pw_ready, 1)
            nc.gpsimd.tensor_tensor(weighted[:, :, :].rearrange("p b (e j) -> p (b e) j", j=CAP),
                                    onehot[:, :, :].rearrange("p b (e j) -> p (b e) j", j=CAP),
                                    pw[:, :].unsqueeze(2).to_broadcast([P, TB * E, CAP]),
                                    ALU.mult).then_inc(weighted_ready, 1)

        @block.vector
        def _(dve):
            steps = [0]

            def step(ins):
                steps[0] += 1
                ins.then_inc(dve_step, 1)
                dve.wait_ge(dve_step, steps[0])

            def norm_stats(b):
                step(nc.vector.bn_stats(stats[:, b], x_sb[:, b]))
                step(nc.vector.bn_aggr(meanvar[:, b], stats[:, b]))
                nc.vector.tensor_scalar(vareps[:, b:b + 1], meanvar[:, b, 1:2], EPS, None,
                                        ALU.add).then_inc(vareps_ready, 1)

            def norm_apply(n, b):
                dve.wait_ge(rstd_ready, TB * n + b + 1)
                nc.vector.tensor_scalar(xn[:, b], x_sb[:, b], meanvar[:, b, 0:1], rstd[:, b:b + 1], ALU.subtract,
                                        ALU.mult).then_inc(xn_ready, 1)

            dve.wait_ge(x_loaded, 16)
            for b in range(TB):
                norm_stats(b)
            for b in range(TB):
                norm_apply(0, b)
            dve.wait_ge(k_hi_ready, 1)
            nc.vector.tensor_tensor(k_lo[:, 0], kT[:, 0], k_hi[:, 0].bitcast(FP32), ALU.subtract).then_inc(k_lo_ready, 1)
            for b in range(TB):
                dve.wait_ge(q_hi_ready, b + 1)
                cols = slice(b * P, (b + 1) * P)
                nc.vector.tensor_tensor(q_lo[:, :, cols], ln_ps[b], q_hi[:, :, cols].bitcast(FP32),
                                        ALU.subtract).then_inc(q_lo_ready, 1)
            dve.wait_ge(rel_ready, 2)
            for h in range(NH):
                nc.vector.tensor_scalar(bias[:, h], rel[:, :], SLOPES[h], None, ALU.mult)

            def lo_of(i, b):
                dve.wait_ge(p_hi_ready, i * 2 + (b + 1))
                nc.vector.tensor_tensor(p_lo[:, b].rearrange("p n q -> p (n q)"), t_bank[b][:, :],
                                        p_hi[:, b].rearrange("p n q -> p (n q)").bitcast(FP32),
                                        ALU.subtract).then_inc(p_lo_ready, 1)

            def first_max(b):
                dve.wait_ge(scores_ready, b + 1)
                nc.vector.tensor_reduce(negmax[:, b, 0:1], s_bank[b][:, :], AX.X, ALU.max,
                                        negate=True).then_inc(negmax_ready, 1)

            def next_max(i, b):
                dve.wait_ge(scores_ready, i * 2 + (b + 1))
                nc.vector.tensor_reduce(chunkneg[:, b:b + 1], s_bank[b][:, :], AX.X, ALU.max,
                                        negate=True).then_inc(chunkmax_ready, 1)
                dve.wait_ge(chunkmax_ready, i * 2 + (b - 1))
                nc.vector.tensor_tensor(negmax[:, b, bass.ds(i, 1)], chunkneg[:, b:b + 1],
                                        negmax[:, b, bass.ds(i - 1, 1)], ALU.min).then_inc(negmax_ready, 1)

            def first_out(b):
                dve.wait_ge(probs_ready, b + 1)
                nc.vector.tensor_copy(denom[:, b:b + 1], rowsum[:, b, 0:1]).then_inc(denom_ready, 1)
                dve.wait_ge(chunk_out_ready, b + 1)
                nc.vector.tensor_copy(acc[:, b], o_bank[b][:, 0:C]).then_inc(acc_ready, 1)

            def next_out(i, b):
                dve.wait_ge(shrink_ready, i * 2 + (b - 1))
                dve.wait_ge(probs_ready, i * 2 + (b + 1))
                dve.wait_ge(denom_ready, i * 2 + (b - 1))
                nc.vector.scalar_tensor_tensor(denom[:, b:b + 1], denom[:, b:b + 1], shrink[:, b, bass.ds(i, 1)],
                                               rowsum[:, b, bass.ds(i, 1)], ALU.mult,
                                               ALU.add).then_inc(denom_ready, 1)
                dve.wait_ge(chunk_out_ready, i * 2 + (b + 1))
                dve.wait_ge(acc_ready, i * 2 + (b - 1))
                nc.vector.scalar_tensor_tensor(acc[:, b], acc[:, b], shrink[:, b, bass.ds(i, 1)],
                                               o_bank[b][:, 0:C], ALU.mult, ALU.add).then_inc(acc_ready, 1)

            for b in range(TB):
                first_max(b)
            lo_of(0, 0)
            next_max(1, 0)
            lo_of(0, 1)
            first_out(0)
            next_max(1, 1)
            lo_of(1, 0)
            first_out(1)
            next_max(2, 0)
            lo_of(1, 1)
            next_out(1, 0)
            next_max(2, 1)
            with dve.Fori(2, NCH - 1) as i:
                lo_of(i, 0)
                next_out(i - 1, 1)
                next_max(i + 1, 0)
                lo_of(i, 1)
                next_out(i, 0)
                next_max(i + 1, 1)
            lo_of(NCH - 1, 0)
            next_out(NCH - 2, 1)
            lo_of(NCH - 1, 1)

            def add_attention(b):
                dve.wait_ge(denom_ready, TB * (NCH - 1) + b + 1)
                step(nc.vector.reciprocal(rdenom[:, b:b + 1], denom[:, b:b + 1]))
                dve.wait_ge(acc_ready, TB * (NCH - 1) + b + 1)
                step(nc.vector.scalar_tensor_tensor(x_sb[:, b], acc[:, b], rdenom[:, b:b + 1], x_sb[:, b], ALU.mult,
                                                    ALU.add))

            next_out(NCH - 1, 0)
            add_attention(0)
            norm_stats(0)
            next_out(NCH - 1, 1)
            norm_apply(1, 0)
            add_attention(1)
            norm_stats(1)
            norm_apply(1, 1)

            dve.wait_ge(k_plain_ready, TB)
            dve.wait_ge(consts_ready, 3)

            def mask_k(g):
                for h in range(4 * g, 4 * g + 4):
                    nc.vector.tensor_scalar(kM[:, h], k_plain[:, h // HPT], headmask[:, h % HPT:h % HPT + 1], None,
                                            ALU.mult).then_inc(kM_ready[g], 1)

            def bias_unit(n):
                g, b, heads, keys = units(n)
                dve.wait_ge(ascores_ready, n + 1)
                if n >= 3:
                    dve.wait_ge(aprobs_ready, n - 2)
                for m, j in enumerate(heads):
                    at = (1 - b) * 2 * P
                    last = nc.vector.tensor_tensor_reduce(
                        out=biased[:, n % 3, m * keys:(m + 1) * keys], in0=as_bank[n % 3][:, m * keys:(m + 1) * keys],
                        in1=bias[:, 4 * g + j, at:at + keys], scale=-1.0, scalar=-MASKED, op0=ALU.add, op1=ALU.min,
                        accum_out=nmax[:, n, m:m + 1])
                last.then_inc(biased_ready, 1)

            def copy_q0(g):
                n = 3 * g
                dve.wait_ge(aprobsT_in_psum, n + 1)
                if g >= 2:
                    dve.wait_ge(y_in_psum, g - 1)
                nc.vector.tensor_copy(aprobsT[:, g % 2, :, 0], at_bank[n % 2][:, :].rearrange(
                    "p (h q) -> p h q", h=4)).then_inc(aprobsT_q0_ready, 1)

            def spread_sums(g):
                dve.wait_ge(aprobs_ready, 3 * g + 3)
                step(nc.vector.reciprocal(rsum[:, :, :], asum[:, g]))
                if g:
                    dve.wait_ge(y_in_psum, g)
                nc.vector.tensor_copy(rwide[:, :, :, :], rsum[:, :, :].unsqueeze(3).to_broadcast(
                    [P, TB, 4, 32])).then_inc(rwide_ready, 1)

            def normalize_y(g):
                dve.wait_ge(y_in_psum, g + 1)
                step(nc.vector.tensor_copy(r_T[:, :], r_ps))
                nc.vector.tensor_tensor(y_T[:, g], y_ps, r_T[:, :], ALU.mult).then_inc(y_T_ready, 1)
                dve.wait_ge(y_T_ready, g + 1)

            mask_k(0)
            for n in range(NU + 4):
                if n < NU:
                    bias_unit(n)
                if n == 1:
                    mask_k(2)
                if n >= 2 and (n - 2) % 3 == 0 and (n - 2) // 3 < NG:
                    copy_q0((n - 2) // 3)
                if n >= 3 and n % 3 == 0 and n // 3 <= NG:
                    spread_sums(n // 3 - 1)
                if n >= 5 and (n - 5) % 3 == 0:
                    normalize_y((n - 5) // 3)

            for b in range(TB):
                dve.wait_ge(proj_ready, b + 1)
                step(nc.vector.tensor_tensor(x_sb[:, b], proj_ps[b], x_sb[:, b], ALU.add))
                norm_stats(b)
            for b in range(TB):
                norm_apply(2, b)

            dve.wait_ge(router_in_psum, 1)
            nc.vector.tensor_copy(scores[:, :], router_ps)
            step(nc.vector.tensor_copy(work[:, :], router_ps))
            for r in range(CAP // 8):
                best = top[:, 8 * r:8 * r + 8]
                step(nc.vector.max(best, work[:, :]))
                if r == 0:
                    nc.vector.tensor_scalar(negtop[:, :], top[:, 0:1], -1.0, None, ALU.mult).then_inc(negtop_ready, 1)
                step(nc.vector.match_replace(out=work[:, :], in_to_replace=best, in_values=work[:, :],
                                             imm_value=TAKEN))
            step(nc.vector.tensor_scalar(taken[:, :], work[:, :], TAKEN / 2, None, ALU.is_le))
            step(nc.vector.tensor_tensor_scan(place[:, 0], ones_row[:, :], taken[:, :], 0.0, ALU.mult, ALU.add))
            nc.vector.tensor_tensor(place[:, 0], place[:, 0], taken[:, :], ALU.mult).then_inc(place_ready, 1)
            dve.wait_ge(expd_ready, 1)
            nc.vector.tensor_tensor_reduce(out=expd[:, :], in0=expd[:, :], in1=taken[:, :], scale=1.0, scalar=0.0,
                                           op0=ALU.mult, op1=ALU.add, accum_out=wsum[:, :]).then_inc(wsum_ready, 1)
            dve.wait_ge(place_in_psum, 1)
            nc.vector.tensor_tensor(onehot[:, :, :].rearrange("p b (e j) -> p (b e) j", j=CAP),
                                    place_ps[0].unsqueeze(2).to_broadcast([P, TB * E, CAP]),
                                    slot_no[:, :].unsqueeze(1).to_broadcast([P, TB * E, CAP]),
                                    ALU.is_equal).then_inc(onehot_ready, 1)
            dve.wait_ge(wsum_ready, 1)
            step(nc.vector.reciprocal(wsum[:, :], wsum[:, :]))
            nc.vector.tensor_scalar(place[:, 1], expd[:, :], wsum[:, :], None, ALU.mult).then_inc(weight_ready, 1)
            dve.wait_ge(place_in_psum, 2)
            nc.vector.tensor_copy(pw[:, :], place_ps[1]).then_inc(pw_ready, 1)
            dve.wait_ge(xg_in_psum, 2)
            nc.vector.tensor_copy(xg_T[:, 1], xg_ps[1]).then_inc(xg1_ready, 1)
            for g in range(EG):
                dve.wait_ge(silu_ready, g + 1)
                dve.wait_ge(up_in_psum, g + 1)
                nc.vector.tensor_tensor(act[:, g], up_ps[g][1][:, :], act[:, g], ALU.mult).then_inc(act_ready, 1)
            for g in range(EG):
                dve.wait_ge(down_in_psum, g + 1)
                nc.vector.tensor_copy(y_e[:, g], down_ps[g]).then_inc(y_e_ready, 1)
            for b in range(TB):
                dve.wait_ge(moe_in_psum, b + 1)
                nc.vector.tensor_tensor(x_out[:, b], moe_ps[b], x_sb[:, b], ALU.add).then_inc(x_final, 1)

        @block.scalar
        def _(act_eng):
            act_e = act_eng

            def norm_T(n, b):
                act_e.wait_ge(xnT_in_psum, TB * n + b + 1)
                nc.scalar.activation(xnT[:, :, b * P:(b + 1) * P], ln_ps[b], ACT.Copy).then_inc(xnT_ready, 1)

            def split_hi(i, kind):
                if kind == "k":
                    act_e.wait_ge(kT_loaded, i * 16 + 16)
                    nc.scalar.activation(k_hi[:, i % 2], kT[:, i], ACT.Copy).then_inc(k_hi_ready, 1)
                else:
                    act_e.wait_ge(v_loaded, i * 16 + 16)
                    nc.scalar.activation(v_hi[:, i % 2], v_sb[:, i], ACT.Copy).then_inc(v_hi_ready, 1)

            split_hi(0, "k")
            for b in range(TB):
                act_e.wait_ge(xnT_in_psum, b + 1)
                nc.scalar.activation(q_hi[:, :, b * P:(b + 1) * P], ln_ps[b], ACT.Copy).then_inc(q_hi_ready, 1)
            split_hi(0, "v")
            split_hi(1, "k")

            def exps(i, b, first):
                act_e.wait_ge(negmax_ready, i * 2 + (b + 1))
                if not first:
                    act_e.wait_ge(probsT_in_psum, i * 2 + (b - 1))
                nc.scalar.activation(probs[:, b], s_bank[b][:, :], ACT.Exp, bias=negmax[:, b, bass.ds(i, 1)],
                                     accum_out=rowsum[:, b, bass.ds(i, 1)]).then_inc(probs_ready, 1)
                if not first:
                    nc.scalar.activation(shrink[:, b, bass.ds(i, 1)], negmax[:, b, bass.ds(i - 1, 1)], ACT.Exp,
                                         bias=negmax[:, b, bass.ds(i, 1)], scale=-1.0).then_inc(shrink_ready, 1)

            def hi_of(i, b, first=False):
                act_e.wait_ge(probsT_in_psum, i * 2 + (b + 1))
                if not first:
                    act_e.wait_ge(chunk_out_ready, i * 2 + (b - 1))
                nc.scalar.activation(p_hi[:, b].rearrange("p n q -> p (n q)"), t_bank[b][:, :],
                                     ACT.Copy).then_inc(p_hi_ready, 1)

            def next_k(i):
                act_e.wait_ge(scores_ready, i * 2 - 2)
                split_hi(i, "k")

            def next_v(i):
                act_e.wait_ge(chunk_out_ready, i * 2 - 2)
                split_hi(i, "v")

            exps(0, 0, True)
            exps(0, 1, True)
            hi_of(0, 0, True)
            next_k(2)
            hi_of(0, 1, True)
            exps(1, 0, False)
            split_hi(1, "v")
            with act_e.Fori(1, NCH - 2) as i:
                hi_of(i, 0)
                exps(i, 1, False)
                next_k(i + 2)
                hi_of(i, 1)
                exps(i + 1, 0, False)
                next_v(i + 1)
            hi_of(NCH - 2, 0)
            exps(NCH - 2, 1, False)
            hi_of(NCH - 2, 1)
            exps(NCH - 1, 0, False)
            next_v(NCH - 1)
            hi_of(NCH - 1, 0)
            exps(NCH - 1, 1, False)
            hi_of(NCH - 1, 1)

            norm_T(1, 0)
            act_e.wait_ge(vzero_ready, 1)
            for b in range(TB):
                cols = slice(b * P, (b + 1) * P)
                act_e.wait_ge(qkv_in_psum, 3 * b + 1)
                nc.scalar.activation(k_plain[:, :, cols], k_ps[b], ACT.Copy).then_inc(k_plain_ready, 1)
                act_e.wait_ge(qkv_in_psum, 3 * b + 2)
                nc.scalar.activation(q_T[:, :, cols], q_ps[b], ACT.Copy, scale=HD ** -0.5).then_inc(q_ready, 1)
                act_e.wait_ge(qkv_in_psum, 3 * b + 3)
                nc.scalar.activation(vpad[:, b, :, 0:HD], v_ps[b].rearrange("p (h d) -> p h d", h=NH),
                                     ACT.Copy).then_inc(vpad_ready, 1)
                if b == 0:
                    norm_T(1, 1)

            def exp_unit(n):
                g, b, heads, keys = units(n)
                act_e.wait_ge(biased_ready, n + 1)
                if n >= 3:
                    act_e.wait_ge(aprobsT_in_psum, n - 2)
                for m, j in enumerate(heads):
                    last = nc.scalar.activation(aprobs[:, n % 3, m * keys:(m + 1) * keys],
                                                biased[:, n % 3, m * keys:(m + 1) * keys], ACT.Exp,
                                                bias=nmax[:, n, m:m + 1], scale=-1.0,
                                                accum_out=asum[:, g, b, j:j + 1])
                last.then_inc(aprobs_ready, 1)

            def copy_q1(n):
                g, b, heads, keys = units(n)
                act_e.wait_ge(aprobsT_in_psum, n + 1)
                if g >= 2:
                    act_e.wait_ge(y_in_psum, g - 1)
                nc.scalar.activation(aprobsT[:, g % 2, heads[0]:heads[0] + 2, 1:3],
                                     at_bank[n % 2][:, :].rearrange("p (h m q) -> p h m q", h=2, m=2),
                                     ACT.Copy).then_inc(aprobsT_q1_ready, 1)

            for n in range(NU + 1):
                if n < NU:
                    exp_unit(n)
                if n >= 1 and (n - 1) % 3:
                    copy_q1(n - 1)

            for b in range(TB):
                norm_T(2, b)
            act_e.wait_ge(negtop_ready, 1)
            nc.scalar.activation(expd[:, :], scores[:, :], ACT.Exp, bias=negtop[:, :]).then_inc(expd_ready, 1)
            act_e.wait_ge(xg_in_psum, 1)
            nc.scalar.activation(xg_T[:, 0], xg_ps[0], ACT.Copy).then_inc(xg0_ready, 1)
            for g in range(EG):
                act_e.wait_ge(gate_in_psum, g + 1)
                nc.scalar.activation(act[:, g], up_ps[g][0][:, :], ACT.Silu).then_inc(silu_ready, 1)
            act_e.wait_ge(scatter_in_psum, 1)
            nc.scalar.activation(scatter, scatter_ps, ACT.Copy).then_inc(scatter_ready, 1)
            for g in range(EG):
                act_e.wait_ge(hT_in_psum, g + 1)
                nc.scalar.activation(h_T[:, g].rearrange("p k n -> p (k n)"), hT_ps[g][:, :],
                                     ACT.Copy).then_inc(hT_ready, 1)

        @block.tensor
        def _(pe):
            def norm_T(n, b):
                pe.wait_ge(xn_ready, TB * n + b + 1)
                for k in range(KC):
                    last = nc.tensor.transpose(ln_ps[b][:, k], xn[:, b, k * P:(k + 1) * P], ident[:, :])
                last.then_inc(xnT_in_psum, 1)

            pe.wait_ge(ident_ready, 1)
            for b in range(TB):
                norm_T(0, b)

            def scores_of(i, b):
                pe.wait_ge(k_lo_ready, i + 1)
                cols = slice(b * P, (b + 1) * P)
                for k in range(KC):
                    nc.tensor.matmul(s_bank[b][:, :], q_hi[:, k, cols], k_hi[:, i % 2, k], start=(k == 0), stop=False)
                    nc.tensor.matmul(s_bank[b][:, :], q_hi[:, k, cols], k_lo[:, i % 2, k], start=False, stop=False)
                    last = nc.tensor.matmul(s_bank[b][:, :], q_lo[:, k, cols], k_hi[:, i % 2, k], start=False,
                                            stop=(k == KC - 1))
                last.then_inc(scores_ready, 1)

            def transpose_of(i, b, first=False):
                pe.wait_ge(probs_ready, i * 2 + (b + 1))
                if not first:
                    pe.wait_ge(p_lo_ready, i * 2 + (b - 1))
                for n in range(NT):
                    last = nc.tensor.transpose(t_bank[b][:, n * P:(n + 1) * P], probs[:, b, n * P:(n + 1) * P],
                                               ident[:, :])
                last.then_inc(probsT_in_psum, 1)

            def values_of(i, b, first=False):
                pe.wait_ge(p_lo_ready, i * 2 + (b + 1))
                pe.wait_ge(v_lo_ready, i + 1)
                if not first:
                    pe.wait_ge(acc_ready, i * 2 + (b - 1))
                for n in range(NT):
                    nc.tensor.matmul(o_bank[b][:, 0:C], p_hi[:, b, n], v_hi[:, i % 2, n], start=(n == 0), stop=False)
                    nc.tensor.matmul(o_bank[b][:, 0:C], p_hi[:, b, n], v_lo[:, i % 2, n], start=False, stop=False)
                    last = nc.tensor.matmul(o_bank[b][:, 0:C], p_lo[:, b, n], v_hi[:, i % 2, n], start=False,
                                            stop=(n == NT - 1))
                last.then_inc(chunk_out_ready, 1)

            for b in range(TB):
                pe.wait_ge(q_lo_ready, b + 1)
                scores_of(0, b)
            transpose_of(0, 0, True)
            scores_of(1, 0)
            transpose_of(0, 1, True)
            values_of(0, 0, True)
            scores_of(1, 1)
            transpose_of(1, 0)
            values_of(0, 1, True)
            scores_of(2, 0)
            transpose_of(1, 1)
            values_of(1, 0)
            scores_of(2, 1)
            with pe.Fori(2, NCH - 1) as i:
                transpose_of(i, 0)
                values_of(i - 1, 1)
                scores_of(i + 1, 0)
                transpose_of(i, 1)
                values_of(i, 0)
                scores_of(i + 1, 1)
            transpose_of(NCH - 1, 0)
            values_of(NCH - 2, 1)
            transpose_of(NCH - 1, 1)
            for b in range(TB):
                values_of(NCH - 1, b)

            norm_T(1, 0)
            pe.wait_ge(wqkv_loaded, 16)
            pe.wait_ge(p_lo_ready, TB * NCH)
            for b in range(TB):
                pe.wait_ge(xnT_ready, b + 1)
                cols = slice(b * P, (b + 1) * P)
                for which, ps in ((1, k_ps), (0, q_ps)):
                    for m in range(2):
                        for k in range(KC):
                            at = which * C + m * P
                            last = nc.tensor.matmul(ps[b][:, m], wqkv_sb[:, k, at:at + P], xnT[:, k, cols],
                                                    start=(k == 0), stop=(k == KC - 1))
                    last.then_inc(qkv_in_psum, 1)
                if b == 0:
                    norm_T(1, 1)
                for k in range(KC):
                    last = nc.tensor.matmul(v_ps[b], xnT[:, k, cols], wqkv_sb[:, k, 2 * C:3 * C],
                                            start=(k == 0), stop=(k == KC - 1))
                last.then_inc(qkv_in_psum, 1)

            def scores_unit(n):
                g, b, heads, keys = units(n)
                if n == 0:
                    pe.wait_ge(q_ready, TB)
                if n % 3 == 0:
                    pe.wait_ge(kM_ready[g], 4)
                if n >= 3:
                    pe.wait_ge(biased_ready, n - 2)
                h = 4 * g + heads[0]
                nc.tensor.matmul(as_bank[n % 3][:, :], q_T[:, h // HPT, b * P:(b + 1) * P],
                                 kM[:, h:h + len(heads), 0:keys], start=True, stop=True).then_inc(ascores_ready, 1)

            def transpose_unit(n):
                pe.wait_ge(aprobs_ready, n + 1)
                if n == 0:
                    pe.wait_ge(vpad_ready, TB)
                if n >= 2:
                    if (n - 2) % 3 == 0:
                        pe.wait_ge(aprobsT_q0_ready, (n - 2) // 3 + 1)
                    else:
                        pe.wait_ge(aprobsT_q1_ready, 2 * ((n - 2) // 3) + (n - 2) % 3)
                for m in range(4):
                    last = nc.tensor.transpose(at_bank[n % 2][:, m * P:(m + 1) * P],
                                               aprobs[:, n % 3, m * P:(m + 1) * P], ident[:, :])
                last.then_inc(aprobsT_in_psum, 1)

            def values_group(g):
                pe.wait_ge(aprobsT_q0_ready, g + 1)
                pe.wait_ge(aprobsT_q1_ready, 2 * g + 2)
                if g:
                    pe.wait_ge(y_T_ready, g)
                pe.wait_ge(rwide_ready, g + 1)
                for b in range(TB):
                    nc.tensor.transpose(r_ps[:, b * P:(b + 1) * P], rwide[:, b].rearrange("p j d -> p (j d)"),
                                        ident[:, :])
                for j in range(4):
                    nc.tensor.matmul(y_ps[32 * j:32 * j + 32, :], vpad[:, 0, 4 * g + j],
                                     aprobsT[:, g % 2, j, 0:2].rearrange("p m q -> p (m q)"), start=True, stop=False)
                for j in range(4):
                    last = nc.tensor.matmul(y_ps[32 * j:32 * j + 32, P:2 * P], vpad[:, 1, 4 * g + j],
                                            aprobsT[:, g % 2, j, 2], start=False, stop=True)
                last.then_inc(y_in_psum, 1)

            def project(g):
                pe.wait_ge(y_T_ready, g + 1)
                if g == 0:
                    pe.wait_ge(wproj_loaded, 16)
                for b in range(TB):
                    last = nc.tensor.matmul(proj_ps[b], y_T[:, g, b * P:(b + 1) * P], wproj_sb[:, g],
                                            start=(g == 0), stop=(g == NG - 1))
                    if g == NG - 1:
                        last.then_inc(proj_ready, 1)

            for n in range(3):
                scores_unit(n)
            for n in range(NU + 4):
                if 3 <= n + 2 < NU:
                    scores_unit(n + 2)
                if n < NU:
                    transpose_unit(n)
                if n >= 3 and n % 3 == 0 and n // 3 - 1 < NG:
                    values_group(n // 3 - 1)
                if n >= 5 and (n - 5) % 3 == 0:
                    project((n - 5) // 3)

            for b in range(TB):
                norm_T(2, b)
            pe.wait_ge(wg_loaded, 16)
            for b in range(TB):
                pe.wait_ge(xnT_ready, TB + b + 1)
                cols = slice(b * P, (b + 1) * P)
                for k in range(KC):
                    last = nc.tensor.matmul(router_ps[:, cols], wg_sb[:, k], xnT[:, k, cols], start=(k == 0),
                                            stop=(k == KC - 1))
            last.then_inc(router_in_psum, 1)

            def place_T(a):
                for b in range(TB):
                    last = nc.tensor.transpose(place_ps[a][:, b * E:(b + 1) * E], place[:, a, b * P:(b + 1) * P],
                                               ident[0:E, 0:E])
                last.then_inc(place_in_psum, 1)

            pe.wait_ge(place_ready, 1)
            place_T(0)
            pe.wait_ge(onehot_ready, 1)
            for k in range(KC):
                for b in range(TB):
                    last = nc.tensor.matmul(xg_ps[k], xn[:, b, k * P:(k + 1) * P], onehot[:, b],
                                            start=(b == 0), stop=(b == TB - 1))
                last.then_inc(xg_in_psum, 1)
            pe.wait_ge(weight_ready, 1)
            place_T(1)
            pe.wait_ge(xg0_ready, 1)
            pe.wait_ge(xg1_ready, 1)
            pe.wait_ge(pw_ready, 1)
            for g in range(EG):
                pe.wait_ge(wup_loaded[g], 16)
                for w, ready in ((0, gate_in_psum), (1, up_in_psum)):
                    for k in range(KC):
                        for j in range(4):
                            e = 4 * g + j
                            last = nc.tensor.matmul(up_ps[g][w][32 * j:32 * j + 32, :],
                                                    xg_T[:, k, e * CAP:(e + 1) * CAP], wup_sb[:, e, w, k],
                                                    start=(k == 0), stop=(k == KC - 1))
                    last.then_inc(ready, 1)
            pe.wait_ge(weighted_ready, 1)
            for g in range(EG):
                for b in range(TB):
                    last = nc.tensor.transpose(scatter_ps[:, g, b], weighted[:, b, g * P:(g + 1) * P], ident[:, :])
            last.then_inc(scatter_in_psum, 1)
            for g in range(EG):
                pe.wait_ge(act_ready, g + 1)
                if g == 1:
                    pe.wait_ge(scatter_ready, 1)
                for k in range(KH):
                    last = nc.tensor.transpose(hT_ps[g][:, k * P:(k + 1) * P], act[:, g, k * P:(k + 1) * P],
                                               ident[:, :])
                last.then_inc(hT_in_psum, 1)
                pe.wait_ge(hT_ready, g + 1)
                pe.wait_ge(wdn_loaded[g], 16)
                for k in range(KH):
                    for j in range(4):
                        last = nc.tensor.matmul(down_ps[g][32 * j:32 * j + 32, :], h_T[:, g, k, 32 * j:32 * j + 32],
                                                wdn_sb[:, 4 * g + j, k], start=(k == 0), stop=(k == KH - 1))
                last.then_inc(down_in_psum, 1)
            pe.wait_ge(scatter_ready, 1)
            for b in range(TB):
                for g in range(EG):
                    pe.wait_ge(y_e_ready, g + 1)
                    last = nc.tensor.matmul(moe_ps[b], scatter[:, g, b], y_e[:, g], start=(g == 0),
                                            stop=(g == EG - 1))
                last.then_inc(moe_in_psum, 1)


def kernel(x, ctx_1024, L0_attn_w_attn, L0_attn_w_proj, L0_ffn_Wg, L0_ffn_W1, L0_ffn_W2, L0_ffn_W3):
    import numpy as np
    import concourse.bacc as bacc
    from concourse.bass_utils import run_bass_kernel_spmd

    def rows(a, n):
        return a.reshape(n, P, -1).transpose(1, 0, 2)

    ctx = np.asarray(ctx_1024)[0]
    w_proj = np.asarray(L0_attn_w_proj)
    padded = np.zeros((P, NG, C), w_proj.dtype)
    padded.reshape(4, 32, NG, C)[:, 0:HD] = w_proj.T.reshape(NG, 4, HD, C).transpose(1, 2, 0, 3)
    up = [np.asarray(w).transpose(2, 0, 1).reshape(KC, P, E, H).transpose(1, 2, 0, 3)
          for w in (L0_ffn_W1, L0_ffn_W3)]
    arrays = {
        "x_in": rows(np.asarray(x)[0], TB),
        "ctx_t": ctx.reshape(NCH, CH, KC, P).transpose(0, 3, 2, 1),
        "ctx_v": ctx.reshape(NCH, NT, P, C).transpose(0, 2, 1, 3),
        "w_qkv": rows(np.asarray(L0_attn_w_attn).T, KC),
        "w_proj": padded,
        "w_gate": rows(np.asarray(L0_ffn_Wg).T, KC),
        "w_up": np.stack(up, axis=2),
        "w_down": np.asarray(L0_ffn_W2).transpose(2, 0, 1).reshape(KH, P, E, C).transpose(1, 2, 0, 3),
    }
    arrays = {k: np.ascontiguousarray(a) for k, a in arrays.items()}
    nc = bacc.Bacc("TRN2", target_bir_lowering=False, num_devices=1)
    aps = [nc.dram_tensor(k, a.shape, mybir.dt.from_np(a.dtype), kind="ExternalInput").ap()
           for k, a in arrays.items()]
    aps.append(nc.dram_tensor("x_out_dram", (P, TB, C), FP32, kind="ExternalOutput").ap())
    build(nc, *aps)
    r = run_bass_kernel_spmd(nc, [arrays], core_ids=[0])
    return r.results[0]["x_out_dram"].transpose(1, 0, 2).reshape(1, T, C)
```

```python
from contextlib import ExitStack

import concourse.bass as bass
import concourse.mybir as mybir

FP32 = mybir.dt.float32
FP32R = mybir.dt.float32r
ALU = mybir.AluOpType
ACT = mybir.ActivationFunctionType
AX = mybir.AxisListType

P = 128
T, C, S = 256, 256, 4096
TB, KC = T // P, C // P
CH = 512
NCH = S // CH
L = NCH - 1
NT = CH // P
NH, HD = 16, 16
NG = NH // 4
HPT = P // HD
NO = NH // HPT
E, H, CAP = 8, 512, 32
KH = H // P
EG = E // 4
EPS = 1e-5
MASKED = -1e30
TAKEN = -3e38
SLOPES = [2.0 ** (-0.5 * (h + 1)) for h in range(NH)]

WARM_BEFORE_NORM_0 = 9
WARM_BEFORE_SCORES = 3
WARM_BEFORE_NORM_1 = 3
WARM_BEFORE_NORM_2 = 8
WARM_PER_ROUND = 4
EARLY_BIASES, MORE_BIASES, LATE_BIASES = 3, 7, 12


def units(n):
    g, kind = n // 3, n % 3
    return (g, 0, range(0, 4), P) if kind == 0 else (g, 1, range(2 * kind - 2, 2 * kind), 2 * P)


NU = 3 * NG
VECTOR_COPIES = (0, 3, 6, 8, 9)



def build(nc, x, ctx_t, ctx_v, w_qkv, w_proj, w_gate, w_up, w_down, out):
    es = ExitStack()
    with es:
        def sb(name, shape, dtype=FP32):
            return es.enter_context(nc.sbuf_tensor(name, shape, dtype))

        def carve(region, size, pattern, **axes):
            part = region[0][:, region[1]:region[1] + size]
            region[1] += size
            return part.rearrange(pattern, **axes)

        def sem(name):
            return es.enter_context(nc.semaphore(name))

        x_sb = sb("x_sb", [P, TB, C])
        v_sb = sb("v_sb", [P, NCH, NT, C])
        wqkv_sb = sb("wqkv_sb", [P, KC, 3 * C])
        wproj_sb = sb("wproj_sb", [P, NO, C])
        wg_sb = sb("wg_sb", [P, KC, E])
        wup_sb = sb("wup_sb", [P, E, 2, KC, H])
        wdn_sb = sb("wdn_sb", [P, E, KH, C])
        kT = wdn_sb[:, :, :, :].rearrange("p e k c -> p (e k c)").rearrange("p (i k s) -> p i k s", i=NCH, k=KC)
        ident = sb("ident", [P, P])
        power = sb("power", [P, 1])
        headmask = sb("headmask", [P, HPT])
        slot_no = sb("slot_no", [P, CAP])
        ones_row = sb("ones_row", [E, T])
        stats = sb("stats", [P, TB, 6])
        meanvar = sb("meanvar", [P, TB, 2])
        vareps = sb("vareps", [P, TB])
        rstd = sb("rstd", [P, TB])
        xn = sb("xn", [P, TB, C])
        xnT = sb("xnT", [P, KC, T])
        negmax = sb("negmax", [P, TB, NCH])
        chunkneg = sb("chunkneg", [P, TB])
        shrink = sb("shrink", [P, TB, NCH])
        rowsum = sb("rowsum", [P, TB, NCH])
        denom = sb("denom", [P, TB])
        rdenom = sb("rdenom", [P, TB])
        acc = sb("acc", [P, TB, C])
        q_hi = sb("q_hi", [P, KC, T], FP32R)
        q_lo = sb("q_lo", [P, KC, T], FP32R)
        k_hi = sb("k_hi", [P, 2, KC, CH], FP32R)
        k_lo = sb("k_lo", [P, 2, KC, CH], FP32R)
        v_hi = sb("v_hi", [P, 2, NT, C], FP32R)
        v_lo = sb("v_lo", [P, 2, NT, C], FP32R)
        p_hi = sb("p_hi", [P, TB, NT, P], FP32R)
        p_lo = sb("p_lo", [P, TB, NT, P], FP32R)
        before_up = [wup_sb[:, 4:8].rearrange("p e w k h -> p (e w k h)"), 0]
        before_dn = [wdn_sb[:, 4:8].rearrange("p e k c -> p (e k c)"), 0]
        over_v = [v_sb[:, :, :, :].rearrange("p i n c -> p (i n c)"), 0]
        bias = carve(before_up, NH * 3 * P, "p (h k) -> p h k", h=NH)
        probs = before_up[0][:, before_up[1]:before_up[1] + TB * CH].rearrange("p (b k) -> p b k", b=TB)
        biased = carve(before_up, 3 * 512, "p (s k) -> p s k", s=3)
        aprobsT = carve(before_dn, 2 * 4 * 3 * P, "p (s h m q) -> p s h m q", s=2, h=4, m=3)
        y_T = carve(before_dn, NO * T, "p (o t) -> p o t", o=NO)
        kM = carve(over_v, NH * T, "p (h k) -> p h k", h=NH)
        k_plain = carve(over_v, 2 * T, "p (m t) -> p m t", m=2)
        UW = 32 * NH // 2
        vpad = carve(over_v, TB * 2 * (UW + HD), "p (k n) -> p k n", k=TB)
        v_slots = [vpad[:, b].rearrange("p (u n) -> p u n", u=2)[:, :, 0:UW].rearrange(
            "p u (m d) -> p u m d", d=32)[:, :, :, 0:HD] for b in range(TB)]
        aprobs = carve(over_v, 3 * 512, "p (s k) -> p s k", s=3)
        q_T = carve(over_v, 2 * T, "p (m t) -> p m t", m=2)
        nmax = sb("nmax", [P, NU, 4])
        asum = sb("asum", [P, NO, TB, 4, 2])
        rsum = sb("rsum", [P, NO, TB, HPT])
        rwide = sb("rwide", [P, TB, HPT, HD])
        r_T = sb("r_T", [P, NO, T])
        rel = sb("rel", [P, 3 * P])

        scores = sb("scores", [E, T])
        work = sb("work", [E, T])
        top = sb("top", [E, CAP])
        negtop = sb("negtop", [E, 1])
        expd = sb("expd", [E, T])
        taken = sb("taken", [E, T])
        place = sb("place", [E, 2, T])
        wsum = sb("wsum", [E, 1])
        pw = sb("pw", [P, TB * E])
        over_v[1] = 0
        xn_hi, xn_lo = (q[:, :, :].rearrange("p k t -> p (k t)").rearrange("p (b c) -> p b c", b=TB)
                        for q in (q_hi, q_lo))
        onehot = p_hi[:, 0].rearrange("p n q -> p (n q)").rearrange("p (b n) -> p b n", b=TB)
        weighted = carve(over_v, TB * E * CAP, "p (b n) -> p b n", b=TB)
        scatter = carve(over_v, EG * TB * P, "p (g b t) -> p g b t", g=EG, b=TB)
        xg_T = carve(over_v, KC * E * CAP, "p (k n) -> p k n", k=KC)
        act = carve(over_v, EG * H, "p (g h) -> p g h", g=EG)
        h_T = carve(over_v, EG * KH * P, "p (g k n) -> p g k n", g=EG, k=KH)
        y_e = carve(over_v, EG * C, "p (g c) -> p g c", g=EG)
        x_out = carve(over_v, TB * C, "p (b c) -> p b c", b=TB)

        banks = [es.enter_context(nc.psum_tensor(f"bank{i}", [P, 512], FP32)) for i in range(8)]
        s_bank, t_bank, o_bank = banks[0:2], banks[4:6], banks[6:8]
        ln_ps = [banks[2 + b][:, 0:C].rearrange("p (k t) -> p k t", k=KC) for b in range(TB)]
        k_ps, q_ps = ([banks[i][:, 0:C].rearrange("p (m t) -> p m t", m=2) for i in pair] for pair in ((1, 6), (0, 5)))
        v_ps = [banks[i][:, 0:C] for i in (4, 3)]
        as_bank = [banks[0], banks[1], banks[6]]
        at_bank = [banks[7], banks[2]]
        y_ps, r_ps = ([bank[:, at:at + P] for bank in banks[4:6]] for at in (0, P))
        proj_ps = [banks[3][:, 0:C], banks[0][:, 0:C]]

        router_ps = banks[0][0:E, 0:T]
        place_ps = [banks[1][:, 0:TB * E], banks[4][:, 0:TB * E]]
        xg_ps = [banks[3][:, 0:E * CAP], banks[2][:, 0:E * CAP]]
        scatter_ps = banks[0][:, :].rearrange("p (g b t) -> p g b t", g=EG, b=TB)
        up_ps = [[banks[4], banks[5]], [banks[6], banks[7]]]
        hT_ps = [banks[1], banks[0]]
        down_ps = [banks[2][:, 0:C], banks[3][:, 0:C]]
        moe_ps = [banks[4][:, 0:C], banks[5][:, 0:C]]

        x_loaded = sem("x_loaded")
        first_kT_loaded = sem("first_kT_loaded")
        first_v_loaded = sem("first_v_loaded")
        kT_loaded = sem("kT_loaded")
        v_loaded = sem("v_loaded")
        wqkv_loaded = sem("wqkv_loaded")
        wproj_loaded = sem("wproj_loaded")
        wg_loaded = sem("wg_loaded")
        wup_loaded = [sem(f"wup_loaded{g}") for g in range(EG)]
        wdn_loaded = [sem(f"wdn_loaded{g}") for g in range(EG)]
        out_stored = sem("out_stored")
        const_step = sem("const_step")
        ident_ready = sem("ident_ready")
        power_ready = sem("power_ready")
        consts_ready = sem("consts_ready")
        dve_step = sem("dve_step")
        vareps_ready = sem("vareps_ready")
        rstd_ready = sem("rstd_ready")
        xn_ready = sem("xn_ready")
        xnT_in_psum = sem("xnT_in_psum")
        xnT_ready = sem("xnT_ready")
        scores_ready = sem("scores_ready")
        chunkmax_ready = sem("chunkmax_ready")
        negmax_ready = sem("negmax_ready")
        probs_ready = sem("probs_ready")
        shrink_ready = sem("shrink_ready")
        probsT_in_psum = sem("probsT_in_psum")
        q_hi_ready = sem("q_hi_ready")
        q_lo_ready = sem("q_lo_ready")
        k_hi_ready = sem("k_hi_ready")
        first_k_lo_ready = sem("first_k_lo_ready")
        k_lo_ready = sem("k_lo_ready")
        v_hi_ready = sem("v_hi_ready")
        v_lo_ready = sem("v_lo_ready")
        p_hi_ready = sem("p_hi_ready")
        p_lo_ready = sem("p_lo_ready")
        chunk_out_ready = sem("chunk_out_ready")
        denom_ready = sem("denom_ready")
        acc_ready = sem("acc_ready")
        qkv_in_psum = sem("qkv_in_psum")
        q_ready = sem("q_ready")
        k_plain_ready = sem("k_plain_ready")
        vpad_ready = sem("vpad_ready")
        rel_step = sem("rel_step")
        rel_ready = sem("rel_ready")
        vzero_ready = sem("vzero_ready")
        kM_ready = [sem(f"kM_ready{g}") for g in range(NG)]
        rwide_ready = sem("rwide_ready")
        ascores_ready = sem("ascores_ready")
        biased_ready = sem("biased_ready")
        aprobs_ready = sem("aprobs_ready")
        aprobsT_in_psum = sem("aprobsT_in_psum")
        aprobsT_ready = [sem(f"aprobsT{i}_ready") for i in range(3)]
        y_in_psum = sem("y_in_psum")
        y_T_ready = sem("y_T_ready")
        proj_ready = sem("proj_ready")

        router_in_psum = sem("router_in_psum")
        scores_kept = sem("scores_kept")
        round_ready = sem("round_ready")
        xn_hi_ready = sem("xn_hi_ready")
        xn_lo_ready = sem("xn_lo_ready")
        expd_ready = sem("expd_ready")
        place_ready = sem("place_ready")
        weight_ready = sem("weight_ready")
        wsum_ready = sem("wsum_ready")
        place_in_psum = sem("place_in_psum")
        pw_ready = sem("pw_ready")
        onehot_ready = sem("onehot_ready")
        weighted_ready = sem("weighted_ready")
        xg_in_psum = sem("xg_in_psum")
        xg0_ready = sem("xg0_ready")
        xg1_ready = sem("xg1_ready")
        scatter_in_psum = sem("scatter_in_psum")
        scatter_ready = sem("scatter_ready")
        gate_in_psum = sem("gate_in_psum")
        up_in_psum = sem("up_in_psum")
        silu_ready = sem("silu_ready")
        act_ready = sem("act_ready")
        hT_in_psum = sem("hT_in_psum")
        hT_ready = sem("hT_ready")
        down_in_psum = sem("down_in_psum")
        y_e_ready = sem("y_e_ready")
        moe_in_psum = sem("moe_in_psum")
        x_final = sem("x_final")

        def transposed(n):
            g, b, heads, keys = units(n)
            to = aprobsT[:, g % 2, heads[0]:heads[-1] + 1]
            if b == 0:
                return to[:, :, 0], at_bank[n % 2][:, :].rearrange("p (h q) -> p h q", h=4)
            return to[:, :, 1:3], at_bank[n % 2][:, :].rearrange("p (h m q) -> p h m q", h=2, m=2)

        block = es.enter_context(nc.Block())

        @block.sync
        def _(sync):
            sync.dma_start(x_sb[:, :, :], x).then_inc(x_loaded, 16)
            sync.dma_start(kT[:, 0], ctx_t[0]).then_inc(first_kT_loaded, 16)
            sync.dma_start(kT[:, 1], ctx_t[1]).then_inc(kT_loaded, 16)
            sync.dma_start(v_sb[:, 0], ctx_v[0]).then_inc(first_v_loaded, 16)
            sync.dma_start(v_sb[:, 1], ctx_v[1]).then_inc(v_loaded, 16)
            for i in range(2, NCH):
                sync.wait_ge(kT_loaded, (i - 1) * 16)
                sync.dma_start(kT[:, i], ctx_t[i]).then_inc(kT_loaded, 16)
                sync.wait_ge(v_loaded, (i - 1) * 16)
                sync.dma_start(v_sb[:, i], ctx_v[i]).then_inc(v_loaded, 16)
            sync.dma_start(wqkv_sb[:, :, :], w_qkv).then_inc(wqkv_loaded, 16)
            sync.dma_start(wproj_sb[:, :, :], w_proj).then_inc(wproj_loaded, 16)
            sync.dma_start(wg_sb[:, :, :], w_gate).then_inc(wg_loaded, 16)
            sync.dma_start(wup_sb[:, 0:4], w_up[:, 0:4]).then_inc(wup_loaded[0], 16)
            sync.wait_ge(k_lo_ready, NCH)
            sync.dma_start(wdn_sb[:, 0:4], w_down[:, 0:4]).then_inc(wdn_loaded[0], 16)
            sync.wait_ge(aprobs_ready, NU)
            sync.dma_start(wup_sb[:, 4:8], w_up[:, 4:8]).then_inc(wup_loaded[1], 16)
            sync.wait_ge(proj_ready, TB)
            sync.dma_start(wdn_sb[:, 4:8], w_down[:, 4:8]).then_inc(wdn_loaded[1], 16)
            for b in range(TB):
                sync.wait_ge(x_final, b + 1)
                sync.dma_start(out[:, b], x_out[:, b]).then_inc(out_stored, 16)
            sync.wait_ge(out_stored, 16 * TB)

        @block.gpsimd
        def _(pool):
            nc.gpsimd.memset(ident[:, :], 0.0).then_inc(const_step, 1)
            nc.gpsimd.memset(power[:, :], -0.5).then_inc(power_ready, 1)
            pool.wait_ge(const_step, 1)
            nc.gpsimd.affine_select(out=ident[:, :], in_=ident[:, :], compare_op=ALU.not_equal, fill=1.0, base=0,
                                    pattern=[[-1, P]], channel_multiplier=1).then_inc(ident_ready, 1)

            def rstd_of(n, b):
                pool.wait_ge(vareps_ready, TB * n + b + 1)
                nc.gpsimd.tensor_tensor(rstd[:, b:b + 1], vareps[:, b:b + 1], power[:, :],
                                        ALU.pow).then_inc(rstd_ready, 1)

            pool.wait_ge(power_ready, 1)
            for b in range(TB):
                rstd_of(0, b)
            nc.gpsimd.iota(rel[:, 0:2 * P], pattern=[[1, 2 * P]], base=-P, channel_multiplier=-1,
                           allow_small_or_imprecise_dtypes=True).then_inc(rel_step, 1)
            nc.gpsimd.iota(rel[:, 2 * P:], pattern=[[1, P]], base=0, channel_multiplier=-1,
                           allow_small_or_imprecise_dtypes=True).then_inc(rel_step, 1)
            pool.wait_ge(rel_step, 2)
            nc.gpsimd.affine_select(out=rel[:, 0:2 * P], in_=rel[:, 0:2 * P], compare_op=ALU.is_ge, fill=MASKED,
                                    base=P, pattern=[[-1, 2 * P]], channel_multiplier=1).then_inc(rel_ready, 1)
            nc.gpsimd.affine_select(out=rel[:, 2 * P:], in_=rel[:, 2 * P:], compare_op=ALU.is_ge, fill=MASKED,
                                    base=0, pattern=[[-1, P]], channel_multiplier=1).then_inc(rel_ready, 1)
            nc.gpsimd.memset(headmask[:, :], 1.0).then_inc(const_step, 1)
            nc.gpsimd.memset(ones_row[:, :], 1.0).then_inc(consts_ready, 1)
            nc.gpsimd.iota(slot_no[:, :], pattern=[[1, CAP]], base=1, channel_multiplier=0,
                           allow_small_or_imprecise_dtypes=True).then_inc(consts_ready, 1)
            pool.wait_ge(const_step, 2)
            nc.gpsimd.affine_select(out=headmask[:, :], in_=headmask[:, :], compare_op=ALU.is_ge, fill=0.0, base=0,
                                    pattern=[[-HD, HPT]], channel_multiplier=1).then_inc(const_step, 1)
            pool.wait_ge(const_step, 3)
            nc.gpsimd.affine_select(out=headmask[:, :], in_=headmask[:, :], compare_op=ALU.is_ge, fill=0.0,
                                    base=HD - 1, pattern=[[HD, HPT]],
                                    channel_multiplier=-1).then_inc(consts_ready, 1)

            def split_lo(i, kind):
                if kind == "k":
                    pool.wait_ge(k_hi_ready, i + 1)
                    nc.gpsimd.tensor_tensor(k_lo[:, i % 2], kT[:, i], k_hi[:, i % 2].bitcast(FP32),
                                            ALU.subtract).then_inc(k_lo_ready, 1)
                else:
                    pool.wait_ge(v_hi_ready, i + 1)
                    nc.gpsimd.tensor_tensor(v_lo[:, i % 2], v_sb[:, i], v_hi[:, i % 2].bitcast(FP32),
                                            ALU.subtract).then_inc(v_lo_ready, 1)

            pool.wait_ge(k_lo_ready, 1)
            split_lo(1, "k")
            split_lo(0, "v")
            split_lo(2, "k")
            split_lo(1, "v")
            with pool.Fori(1, NCH - 2) as i:
                split_lo(i + 2, "k")
                split_lo(i + 1, "v")
            split_lo(NCH - 1, "v")
            pool.wait_ge(v_lo_ready, NCH)
            nc.gpsimd.memset(vpad[:, :, :], 0.0).then_inc(vzero_ready, 1)
            for b in range(TB):
                rstd_of(1, b)
            pool.wait_ge(consts_ready, 3)
            for g in (1, 3):
                for b in range(TB):
                    pool.wait_ge(k_plain_ready, b + 1)
                    cols = slice(b * P, (b + 1) * P)
                    for h in range(4 * g, 4 * g + 4):
                        nc.gpsimd.tensor_scalar(kM[:, h, cols], k_plain[:, h // HPT, cols],
                                                headmask[:, h % HPT:h % HPT + 1], None,
                                                ALU.mult).then_inc(kM_ready[g], 1)
            for b in range(TB):
                rstd_of(2, b)
            pool.wait_ge(xn_hi_ready, 1)
            nc.gpsimd.tensor_tensor(xn_lo, xn[:, :, :], xn_hi.bitcast(FP32), ALU.subtract).then_inc(xn_lo_ready, 1)
            pool.wait_ge(onehot_ready, TB)
            pool.wait_ge(pw_ready, 1)
            nc.gpsimd.tensor_tensor(weighted[:, :, :].rearrange("p b (e j) -> p (b e) j", j=CAP),
                                    onehot.rearrange("p b (e j) -> p (b e) j", j=CAP).bitcast(FP32),
                                    pw[:, :].unsqueeze(2).to_broadcast([P, TB * E, CAP]),
                                    ALU.mult).then_inc(weighted_ready, 1)

        @block.vector
        def _(dve):
            steps = [0]

            def step(ins):
                steps[0] += 1
                ins.then_inc(dve_step, 1)
                dve.wait_ge(dve_step, steps[0])

            def norm_stats(b):
                step(nc.vector.bn_stats(stats[:, b], x_sb[:, b]))
                step(nc.vector.bn_aggr(meanvar[:, b], stats[:, b]))
                nc.vector.tensor_scalar(vareps[:, b:b + 1], meanvar[:, b, 1:2], EPS, None,
                                        ALU.add).then_inc(vareps_ready, 1)

            def norm_apply(n, b):
                dve.wait_ge(rstd_ready, TB * n + b + 1)
                nc.vector.tensor_scalar(xn[:, b], x_sb[:, b], meanvar[:, b, 0:1], rstd[:, b:b + 1], ALU.subtract,
                                        ALU.mult).then_inc(xn_ready, 1)

            dve.wait_ge(x_loaded, 16)
            for b in range(TB):
                norm_stats(b)
            for b in range(TB):
                norm_apply(0, b)
            dve.wait_ge(k_hi_ready, 1)
            for k, ready in ((0, first_k_lo_ready), (1, k_lo_ready)):
                nc.vector.tensor_tensor(k_lo[:, 0, k], kT[:, 0, k], k_hi[:, 0, k].bitcast(FP32),
                                        ALU.subtract).then_inc(ready, 1)
                b = k
                dve.wait_ge(q_hi_ready, b + 1)
                cols = slice(b * P, (b + 1) * P)
                nc.vector.tensor_tensor(q_lo[:, :, cols], ln_ps[b], q_hi[:, :, cols].bitcast(FP32),
                                        ALU.subtract).then_inc(q_lo_ready, 1)

            def bias_heads(first, end):
                for h in range(first, end):
                    nc.vector.tensor_scalar(bias[:, h], rel[:, :], SLOPES[h], None, ALU.mult)

            dve.wait_ge(rel_ready, 2)
            bias_heads(0, EARLY_BIASES)

            def lo_of(i, b):
                dve.wait_ge(p_hi_ready, i * 2 + (b + 1))
                nc.vector.tensor_tensor(p_lo[:, b].rearrange("p n q -> p (n q)"), t_bank[b][:, :],
                                        p_hi[:, b].rearrange("p n q -> p (n q)").bitcast(FP32),
                                        ALU.subtract).then_inc(p_lo_ready, 1)

            def first_max(b):
                dve.wait_ge(scores_ready, b + 1)
                nc.vector.tensor_reduce(negmax[:, b, 0:1], s_bank[b][:, :], AX.X, ALU.max,
                                        negate=True).then_inc(negmax_ready, 1)

            def next_max(i, b):
                dve.wait_ge(scores_ready, i * 2 + (b + 1))
                nc.vector.tensor_reduce(chunkneg[:, b:b + 1], s_bank[b][:, :], AX.X, ALU.max,
                                        negate=True).then_inc(chunkmax_ready, 1)
                dve.wait_ge(chunkmax_ready, i * 2 + (b - 1))
                nc.vector.tensor_tensor(negmax[:, b, bass.ds(i, 1)], chunkneg[:, b:b + 1],
                                        negmax[:, b, bass.ds(i - 1, 1)], ALU.min).then_inc(negmax_ready, 1)

            def first_out(b):
                dve.wait_ge(probs_ready, b + 1)
                nc.vector.tensor_copy(denom[:, b:b + 1], rowsum[:, b, 0:1]).then_inc(denom_ready, 1)
                dve.wait_ge(chunk_out_ready, b + 1)
                nc.vector.tensor_copy(acc[:, b], o_bank[b][:, 0:C]).then_inc(acc_ready, 1)

            def next_out(i, b):
                dve.wait_ge(shrink_ready, i * 2 + (b - 1))
                dve.wait_ge(probs_ready, i * 2 + (b + 1))
                dve.wait_ge(denom_ready, i * 2 + (b - 1))
                nc.vector.scalar_tensor_tensor(denom[:, b:b + 1], denom[:, b:b + 1], shrink[:, b, bass.ds(i, 1)],
                                               rowsum[:, b, bass.ds(i, 1)], ALU.mult,
                                               ALU.add).then_inc(denom_ready, 1)
                dve.wait_ge(chunk_out_ready, i * 2 + (b + 1))
                dve.wait_ge(acc_ready, i * 2 + (b - 1))
                nc.vector.scalar_tensor_tensor(acc[:, b], acc[:, b], shrink[:, b, bass.ds(i, 1)],
                                               o_bank[b][:, 0:C], ALU.mult, ALU.add).then_inc(acc_ready, 1)

            for b in range(TB):
                first_max(b)
            lo_of(0, 0)
            next_max(1, 0)
            lo_of(0, 1)
            first_out(0)
            next_max(1, 1)
            lo_of(1, 0)
            first_out(1)
            next_max(2, 0)
            lo_of(1, 1)
            next_out(1, 0)
            next_max(2, 1)
            with dve.Fori(2, NCH - 2) as i:
                lo_of(i, 0)
                next_out(i - 1, 1)
                next_max(i + 1, 0)
                lo_of(i, 1)
                next_out(i, 0)
                next_max(i + 1, 1)
            lo_of(L - 1, 0)
            next_out(L - 2, 1)
            next_max(L, 0)
            lo_of(L - 1, 1)
            next_out(L - 1, 0)

            def add_attention(b):
                dve.wait_ge(denom_ready, 2 * L + b + 1)
                step(nc.vector.reciprocal(rdenom[:, b:b + 1], denom[:, b:b + 1]))
                dve.wait_ge(acc_ready, 2 * L + b + 1)
                step(nc.vector.scalar_tensor_tensor(x_sb[:, b], acc[:, b], rdenom[:, b:b + 1], x_sb[:, b], ALU.mult,
                                                    ALU.add))

            lo_of(L, 0)
            next_max(L, 1)
            next_out(L - 1, 1)
            lo_of(L, 1)
            next_out(L, 0)
            add_attention(0)
            norm_stats(0)
            next_out(L, 1)
            norm_apply(1, 0)
            add_attention(1)
            norm_stats(1)
            norm_apply(1, 1)
            bias_heads(EARLY_BIASES, MORE_BIASES)

            dve.wait_ge(consts_ready, 3)

            def mask_k(g, b):
                dve.wait_ge(k_plain_ready, b + 1)
                cols = slice(b * P, (b + 1) * P)
                for h in range(4 * g, 4 * g + 4):
                    nc.vector.tensor_scalar(kM[:, h, cols], k_plain[:, h // HPT, cols],
                                            headmask[:, h % HPT:h % HPT + 1], None, ALU.mult).then_inc(kM_ready[g], 1)

            def bias_unit(n):
                g, b, heads, keys = units(n)
                dve.wait_ge(ascores_ready, n + 1)
                if n >= 3:
                    dve.wait_ge(aprobs_ready, n - 2)
                for m, j in enumerate(heads):
                    at = (1 - b) * 2 * P
                    last = nc.vector.tensor_tensor_reduce(
                        out=biased[:, n % 3, m * keys:(m + 1) * keys], in0=as_bank[n % 3][:, m * keys:(m + 1) * keys],
                        in1=bias[:, 4 * g + j, at:at + keys], scale=-1.0, scalar=-MASKED, op0=ALU.add, op1=ALU.min,
                        accum_out=nmax[:, n, m:m + 1])
                last.then_inc(biased_ready, 1)

            def copy_transposed(n):
                dve.wait_ge(aprobsT_in_psum, n + 1)
                if n >= 6:
                    dve.wait_ge(y_in_psum, TB * (n // 3 - 2) + (1 if n % 3 == 0 else 2))
                nc.vector.tensor_copy(*transposed(n)).then_inc(aprobsT_ready[n % 3], 1)

            def spread_sums(o, b):
                dve.wait_ge(aprobs_ready, 6 * o + (4, 6)[b])
                step(nc.vector.reciprocal(rsum[:, o, b], asum[:, o, b].rearrange("p j u -> p (j u)")))
                if o:
                    dve.wait_ge(y_in_psum, TB * (2 * o - 1) + b + 1)
                nc.vector.tensor_copy(rwide[:, b], rsum[:, o, b].unsqueeze(2).to_broadcast(
                    [P, HPT, HD])).then_inc(rwide_ready, 1)

            def normalize_y(o, b):
                cols = slice(b * P, (b + 1) * P)
                dve.wait_ge(y_in_psum, TB * (2 * o + 1) + b + 1)
                step(nc.vector.tensor_copy(r_T[:, o, cols], r_ps[b]))
                nc.vector.tensor_tensor(y_T[:, o, cols], y_ps[b], r_T[:, o, cols], ALU.mult).then_inc(y_T_ready, 1)

            def add_projected(b):
                dve.wait_ge(proj_ready, b + 1)
                step(nc.vector.tensor_tensor(x_sb[:, b], proj_ps[b], x_sb[:, b], ALU.add))
                norm_stats(b)

            mask_k(0, 0)
            bias_heads(MORE_BIASES, LATE_BIASES)
            mask_k(0, 1)
            for n in range(NU):
                bias_unit(n)
                if n == 3:
                    for b in range(TB):
                        mask_k(2, b)
                if n == 5:
                    bias_heads(LATE_BIASES, NH)
                if n - 2 in VECTOR_COPIES:
                    copy_transposed(n - 2)
                if n > 0 and n % 6 == 0:
                    for b in range(TB):
                        spread_sums(n // 6 - 1, b)
                if n > 6 and n % 6 == 2:
                    for b in range(TB):
                        normalize_y(n // 6 - 1, b)
            for b in range(TB):
                spread_sums(NO - 1, b)
            for b in range(TB):
                normalize_y(NO - 1, b)
            add_projected(0)
            add_projected(1)
            norm_apply(2, 0)
            norm_apply(2, 1)

            dve.wait_ge(router_in_psum, 1)
            for r in range(CAP // 8):
                best = top[:, 8 * r:8 * r + 8]
                left = router_ps if r == 0 else work[:, :]
                step(nc.vector.max(best, left))
                if r == 0:
                    nc.vector.tensor_scalar(negtop[:, :], top[:, 0:1], -1.0, None, ALU.mult)
                nc.vector.match_replace(out=work[:, :], in_to_replace=best, in_values=left,
                                        imm_value=TAKEN).then_inc(round_ready, 1)
                dve.wait_ge(round_ready, r + 1)
                if r == 0:
                    nc.vector.tensor_copy(scores[:, :], router_ps).then_inc(scores_kept, 1)
            step(nc.vector.tensor_scalar(taken[:, :], work[:, :], TAKEN / 2, None, ALU.is_le))
            step(nc.vector.tensor_tensor_scan(place[:, 0], ones_row[:, :], taken[:, :], 0.0, ALU.mult, ALU.add))
            nc.vector.tensor_tensor(place[:, 0], place[:, 0], taken[:, :], ALU.mult).then_inc(place_ready, 1)
            dve.wait_ge(expd_ready, 1)
            nc.vector.tensor_tensor_reduce(out=expd[:, :], in0=expd[:, :], in1=taken[:, :], scale=1.0, scalar=0.0,
                                           op0=ALU.mult, op1=ALU.add, accum_out=wsum[:, :]).then_inc(wsum_ready, 1)
            dve.wait_ge(place_in_psum, 1)
            for b in range(TB):
                nc.vector.tensor_tensor(onehot[:, b].rearrange("p (e j) -> p e j", j=CAP),
                                        place_ps[0][:, b * E:(b + 1) * E].unsqueeze(2).to_broadcast([P, E, CAP]),
                                        slot_no[:, :].unsqueeze(1).to_broadcast([P, E, CAP]),
                                        ALU.is_equal).then_inc(onehot_ready, 1)
            dve.wait_ge(wsum_ready, 1)
            step(nc.vector.reciprocal(wsum[:, :], wsum[:, :]))
            nc.vector.tensor_scalar(place[:, 1], expd[:, :], wsum[:, :], None, ALU.mult).then_inc(weight_ready, 1)
            dve.wait_ge(place_in_psum, 2)
            nc.vector.tensor_copy(pw[:, :], place_ps[1]).then_inc(pw_ready, 1)
            dve.wait_ge(xg_in_psum, 2)
            nc.vector.tensor_copy(xg_T[:, 1], xg_ps[1]).then_inc(xg1_ready, 1)
            for g in range(EG):
                dve.wait_ge(silu_ready, g + 1)
                dve.wait_ge(up_in_psum, g + 1)
                nc.vector.tensor_tensor(act[:, g], up_ps[g][1][:, :], act[:, g], ALU.mult).then_inc(act_ready, 1)
            for g in range(EG):
                dve.wait_ge(down_in_psum, g + 1)
                nc.vector.tensor_copy(y_e[:, g], down_ps[g]).then_inc(y_e_ready, 1)
            for b in range(TB):
                dve.wait_ge(moe_in_psum, b + 1)
                nc.vector.tensor_tensor(x_out[:, b], moe_ps[b], x_sb[:, b], ALU.add).then_inc(x_final, 1)

        @block.scalar
        def _(scalar):
            def norm_T(n, b):
                scalar.wait_ge(xnT_in_psum, TB * n + b + 1)
                nc.scalar.activation(xnT[:, :, b * P:(b + 1) * P], ln_ps[b], ACT.Copy).then_inc(xnT_ready, 1)

            def split_k(i, first=False):
                scalar.wait_ge(first_kT_loaded if first else kT_loaded, 16 if first else i * 16)
                nc.scalar.activation(k_hi[:, i % 2], kT[:, i], ACT.Copy).then_inc(k_hi_ready, 1)

            def split_v(i, first=False):
                scalar.wait_ge(first_v_loaded if first else v_loaded, 16 if first else i * 16)
                nc.scalar.activation(v_hi[:, i % 2], v_sb[:, i], ACT.Copy).then_inc(v_hi_ready, 1)

            split_k(0, True)
            for b in range(TB):
                scalar.wait_ge(xnT_in_psum, b + 1)
                nc.scalar.activation(q_hi[:, :, b * P:(b + 1) * P], ln_ps[b], ACT.Copy).then_inc(q_hi_ready, 1)
            split_k(1)
            split_v(0, True)

            def exps(i, b, first):
                scalar.wait_ge(negmax_ready, i * 2 + (b + 1))
                if not first:
                    scalar.wait_ge(probsT_in_psum, i * 2 + (b - 1))
                nc.scalar.activation(probs[:, b], s_bank[b][:, :], ACT.Exp, bias=negmax[:, b, bass.ds(i, 1)],
                                     accum_out=rowsum[:, b, bass.ds(i, 1)]).then_inc(probs_ready, 1)
                if not first:
                    nc.scalar.activation(shrink[:, b, bass.ds(i, 1)], negmax[:, b, bass.ds(i - 1, 1)], ACT.Exp,
                                         bias=negmax[:, b, bass.ds(i, 1)], scale=-1.0).then_inc(shrink_ready, 1)

            def hi_of(i, b, first=False):
                scalar.wait_ge(probsT_in_psum, i * 2 + (b + 1))
                if not first:
                    scalar.wait_ge(chunk_out_ready, i * 2 + (b - 1))
                nc.scalar.activation(p_hi[:, b].rearrange("p n q -> p (n q)"), t_bank[b][:, :],
                                     ACT.Copy).then_inc(p_hi_ready, 1)

            def next_k(i):
                scalar.wait_ge(scores_ready, i * 2 - 2)
                split_k(i)

            def next_v(i):
                scalar.wait_ge(chunk_out_ready, i * 2 - 2)
                split_v(i)

            exps(0, 0, True)
            exps(0, 1, True)
            hi_of(0, 0, True)
            next_k(2)
            hi_of(0, 1, True)
            exps(1, 0, False)
            split_v(1)
            with scalar.Fori(1, NCH - 2) as i:
                hi_of(i, 0)
                exps(i, 1, False)
                next_k(i + 2)
                hi_of(i, 1)
                exps(i + 1, 0, False)
                next_v(i + 1)
            hi_of(NCH - 2, 0)
            exps(NCH - 2, 1, False)
            next_v(NCH - 1)
            hi_of(NCH - 2, 1)
            exps(NCH - 1, 0, False)
            hi_of(NCH - 1, 0)
            exps(NCH - 1, 1, False)
            hi_of(NCH - 1, 1)

            norm_T(1, 0)

            def copy_v(b):
                scalar.wait_ge(qkv_in_psum, 3 * b + 3)
                nc.scalar.activation(v_slots[b], v_ps[b].rearrange("p (u m d) -> p u m d", u=2, d=HD),
                                     ACT.Copy).then_inc(vpad_ready, 1)

            scalar.wait_ge(vzero_ready, 1)
            for b in range(TB):
                cols = slice(b * P, (b + 1) * P)
                scalar.wait_ge(qkv_in_psum, 3 * b + 1)
                nc.scalar.activation(k_plain[:, :, cols], k_ps[b], ACT.Copy).then_inc(k_plain_ready, 1)
                if b == 0:
                    norm_T(1, 1)
                scalar.wait_ge(qkv_in_psum, 3 * b + 2)
                nc.scalar.activation(q_T[:, :, cols], q_ps[b], ACT.Copy, scale=HD ** -0.5).then_inc(q_ready, 1)
                if b == 0:
                    copy_v(0)

            def exp_unit(n):
                g, b, heads, keys = units(n)
                scalar.wait_ge(biased_ready, n + 1)
                if n >= 3:
                    scalar.wait_ge(aprobsT_in_psum, n - 2)
                for m, j in enumerate(heads):
                    last = nc.scalar.activation(aprobs[:, n % 3, m * keys:(m + 1) * keys],
                                                biased[:, n % 3, m * keys:(m + 1) * keys], ACT.Exp,
                                                bias=nmax[:, n, m:m + 1], scale=-1.0,
                                                accum_out=asum[:, g // 2, b, j, g % 2:g % 2 + 1])
                last.then_inc(aprobs_ready, 1)

            def copy_transposed(n):
                scalar.wait_ge(aprobsT_in_psum, n + 1)
                if n >= 6:
                    scalar.wait_ge(y_in_psum, TB * (n // 3 - 2) + (1 if n % 3 == 0 else 2))
                to, at = transposed(n)
                nc.scalar.activation(to, at, ACT.Copy).then_inc(aprobsT_ready[n % 3], 1)

            for n in range(NU + 1):
                if n < NU:
                    exp_unit(n)
                if n == 1:
                    copy_v(1)
                if n >= 1 and n - 1 not in VECTOR_COPIES:
                    copy_transposed(n - 1)

            for b in range(TB):
                norm_T(2, b)
            scalar.wait_ge(xn_ready, 3 * TB)
            nc.scalar.activation(xn_hi, xn[:, :, :], ACT.Copy).then_inc(xn_hi_ready, 1)
            scalar.wait_ge(scores_kept, 1)
            nc.scalar.activation(expd[:, :], scores[:, :], ACT.Exp, bias=negtop[:, :]).then_inc(expd_ready, 1)
            scalar.wait_ge(xg_in_psum, 1)
            nc.scalar.activation(xg_T[:, 0], xg_ps[0], ACT.Copy).then_inc(xg0_ready, 1)

            def silu(g):
                scalar.wait_ge(gate_in_psum, g + 1)
                nc.scalar.activation(act[:, g], up_ps[g][0][:, :], ACT.Silu).then_inc(silu_ready, 1)

            def copy_hidden(g):
                scalar.wait_ge(hT_in_psum, g + 1)
                nc.scalar.activation(h_T[:, g].rearrange("p k n -> p (k n)"), hT_ps[g][:, :],
                                     ACT.Copy).then_inc(hT_ready, 1)

            silu(0)
            silu(1)
            copy_hidden(0)
            scalar.wait_ge(scatter_in_psum, 1)
            nc.scalar.activation(scatter, scatter_ps, ACT.Copy).then_inc(scatter_ready, 1)
            copy_hidden(1)

        @block.tensor
        def _(pe):
            def norm_T(n, b):
                pe.wait_ge(xn_ready, TB * n + b + 1)
                for k in range(KC):
                    last = nc.tensor.transpose(ln_ps[b][:, k], xn[:, b, k * P:(k + 1) * P], ident[:, :])
                last.then_inc(xnT_in_psum, 1)

            def keep_warm(bank, times):
                for _ in range(times):
                    nc.tensor.matmul(bank[:, 0:P], ident[:, :], ident[:, :], start=True, stop=True)

            pe.wait_ge(ident_ready, 1)
            keep_warm(banks[7], WARM_BEFORE_NORM_0)
            norm_T(0, 0)
            norm_T(0, 1)
            keep_warm(banks[7], WARM_BEFORE_SCORES)

            def scores_of(i, b, halves=False):
                pe.wait_ge(first_k_lo_ready if halves else k_lo_ready, 1 if halves else i + 1)
                cols = slice(b * P, (b + 1) * P)
                for k in range(KC):
                    if halves and k:
                        pe.wait_ge(k_lo_ready, 1)
                    nc.tensor.matmul(s_bank[b][:, :], q_hi[:, k, cols], k_hi[:, i % 2, k], start=(k == 0), stop=False)
                    nc.tensor.matmul(s_bank[b][:, :], q_hi[:, k, cols], k_lo[:, i % 2, k], start=False, stop=False)
                    last = nc.tensor.matmul(s_bank[b][:, :], q_lo[:, k, cols], k_hi[:, i % 2, k], start=False,
                                            stop=(k == KC - 1))
                last.then_inc(scores_ready, 1)

            def transpose_of(i, b, first=False):
                pe.wait_ge(probs_ready, i * 2 + (b + 1))
                if not first:
                    pe.wait_ge(p_lo_ready, i * 2 + (b - 1))
                for n in range(NT):
                    last = nc.tensor.transpose(t_bank[b][:, n * P:(n + 1) * P], probs[:, b, n * P:(n + 1) * P],
                                               ident[:, :])
                last.then_inc(probsT_in_psum, 1)

            def values_of(i, b, first=False):
                pe.wait_ge(p_lo_ready, i * 2 + (b + 1))
                pe.wait_ge(v_lo_ready, i + 1)
                if not first:
                    pe.wait_ge(acc_ready, i * 2 + (b - 1))
                for n in range(NT):
                    nc.tensor.matmul(o_bank[b][:, 0:C], p_hi[:, b, n], v_hi[:, i % 2, n], start=(n == 0), stop=False)
                    nc.tensor.matmul(o_bank[b][:, 0:C], p_hi[:, b, n], v_lo[:, i % 2, n], start=False, stop=False)
                    last = nc.tensor.matmul(o_bank[b][:, 0:C], p_lo[:, b, n], v_hi[:, i % 2, n], start=False,
                                            stop=(n == NT - 1))
                last.then_inc(chunk_out_ready, 1)

            for b in range(TB):
                pe.wait_ge(q_lo_ready, b + 1)
                scores_of(0, b, b == 0)
            transpose_of(0, 0, True)
            scores_of(1, 0)
            transpose_of(0, 1, True)
            values_of(0, 0, True)
            scores_of(1, 1)
            transpose_of(1, 0)
            values_of(0, 1, True)
            scores_of(2, 0)
            transpose_of(1, 1)
            values_of(1, 0)
            scores_of(2, 1)
            with pe.Fori(2, NCH - 2) as i:
                transpose_of(i, 0)
                values_of(i - 1, 1)
                scores_of(i + 1, 0)
                transpose_of(i, 1)
                values_of(i, 0)
                scores_of(i + 1, 1)
            transpose_of(L - 1, 0)
            values_of(L - 2, 1)
            scores_of(L, 0)
            transpose_of(L - 1, 1)
            values_of(L - 1, 0)
            transpose_of(L, 0)
            scores_of(L, 1)
            values_of(L - 1, 1)
            transpose_of(L, 1)
            values_of(L, 0)
            values_of(L, 1)

            keep_warm(banks[0], WARM_BEFORE_NORM_1)
            norm_T(1, 0)
            pe.wait_ge(wqkv_loaded, 16)
            pe.wait_ge(p_lo_ready, TB * NCH)

            def scores_unit(n):
                g, b, heads, keys = units(n)
                pe.wait_ge(q_ready, b + 1)
                pe.wait_ge(kM_ready[g], 4 * (b + 1))
                if n >= 3:
                    pe.wait_ge(biased_ready, n - 2)
                h = 4 * g + heads[0]
                nc.tensor.matmul(as_bank[n % 3][:, :], q_T[:, h // HPT, b * P:(b + 1) * P],
                                 kM[:, h:h + len(heads), 0:keys], start=True, stop=True).then_inc(ascores_ready, 1)

            def values(b):
                for k in range(KC):
                    last = nc.tensor.matmul(v_ps[b], xnT[:, k, b * P:(b + 1) * P], wqkv_sb[:, k, 2 * C:3 * C],
                                            start=(k == 0), stop=(k == KC - 1))
                last.then_inc(qkv_in_psum, 1)

            for b in range(TB):
                pe.wait_ge(xnT_ready, b + 1)
                cols = slice(b * P, (b + 1) * P)
                for which, ps in ((1, k_ps), (0, q_ps)):
                    for m in range(2):
                        for k in range(KC):
                            at = which * C + m * P
                            last = nc.tensor.matmul(ps[b][:, m], wqkv_sb[:, k, at:at + P], xnT[:, k, cols],
                                                    start=(k == 0), stop=(k == KC - 1))
                    last.then_inc(qkv_in_psum, 1)
                    if b == 0 and not which:
                        norm_T(1, 1)
                if b == 0:
                    values(0)

            def transpose_unit(n):
                pe.wait_ge(aprobs_ready, n + 1)
                if n >= 2:
                    pe.wait_ge(aprobsT_ready[(n - 2) % 3], (n - 2) // 3 + 1)
                for m in range(4):
                    last = nc.tensor.transpose(at_bank[n % 2][:, m * P:(m + 1) * P],
                                               aprobs[:, n % 3, m * P:(m + 1) * P], ident[:, :])
                last.then_inc(aprobsT_in_psum, 1)

            def values_group(g, b):
                o, u = g // 2, g % 2
                if g == 0:
                    pe.wait_ge(vpad_ready, TB)
                for i in ((1, 2) if b else (0,)):
                    pe.wait_ge(aprobsT_ready[i], g + 1)
                if o and not u:
                    pe.wait_ge(y_T_ready, TB * (o - 1) + b + 1)
                for k in range(b + 1):
                    for j in range(4):
                        at = u * UW + 32 * (4 * o + j)
                        last = nc.tensor.matmul(y_ps[b][32 * j:32 * j + 32, :], vpad[:, k, at:at + 32],
                                                aprobsT[:, g % 2, j, b + k], start=(u == 0 and k == 0),
                                                stop=(u == 1 and k == b))
                if u:
                    pe.wait_ge(rwide_ready, TB * o + b + 1)
                    last = nc.tensor.transpose(r_ps[b], rwide[:, b].rearrange("p h d -> p (h d)"), ident[:, :])
                last.then_inc(y_in_psum, 1)

            def project(o, b):
                pe.wait_ge(y_T_ready, TB * o + b + 1)
                last = nc.tensor.matmul(proj_ps[b], y_T[:, o, b * P:(b + 1) * P], wproj_sb[:, o],
                                        start=(o == 0), stop=(o == NO - 1))
                if o == NO - 1:
                    last.then_inc(proj_ready, 1)

            for n in range(3):
                scores_unit(n)
            values(1)
            for n in range(NU):
                if 3 <= n + 2 < NU:
                    scores_unit(n + 2)
                transpose_unit(n)
                if n >= 3 and n % 3 == 0:
                    for b in range(TB):
                        values_group(n // 3 - 1, b)
            values_group(NG - 1, 0)
            pe.wait_ge(wproj_loaded, 16)
            for o in range(NO - 1):
                project(o, 0)
            values_group(NG - 1, 1)
            project(NO - 1, 0)
            for o in range(NO):
                project(o, 1)

            keep_warm(banks[6], WARM_BEFORE_NORM_2)
            for b in range(TB):
                norm_T(2, b)
            pe.wait_ge(wg_loaded, 16)
            for b in range(TB):
                pe.wait_ge(xnT_ready, TB + b + 1)
                cols = slice(b * P, (b + 1) * P)
                for k in range(KC):
                    last = nc.tensor.matmul(router_ps[:, cols], wg_sb[:, k], xnT[:, k, cols], start=(k == 0),
                                            stop=(k == KC - 1))
            last.then_inc(router_in_psum, 1)

            def place_T(a):
                for b in range(TB):
                    last = nc.tensor.transpose(place_ps[a][:, b * E:(b + 1) * E], place[:, a, b * P:(b + 1) * P],
                                               ident[0:E, 0:E])
                last.then_inc(place_in_psum, 1)

            for r in range(CAP // 8):
                keep_warm(banks[6], WARM_PER_ROUND)
                pe.wait_ge(round_ready, r + 1)
            keep_warm(banks[6], WARM_PER_ROUND)
            pe.wait_ge(place_ready, 1)
            place_T(0)
            pe.wait_ge(xn_lo_ready, 1)
            for b in range(TB):
                pe.wait_ge(onehot_ready, b + 1)
                for k in range(KC):
                    for part in (xn_hi, xn_lo):
                        last = nc.tensor.matmul(xg_ps[k], part[:, b, k * P:(k + 1) * P], onehot[:, b],
                                                start=(b == 0 and part is xn_hi),
                                                stop=(b == TB - 1 and part is xn_lo))
                    if b == TB - 1:
                        last.then_inc(xg_in_psum, 1)
            pe.wait_ge(weight_ready, 1)
            place_T(1)
            pe.wait_ge(xg0_ready, 1)
            pe.wait_ge(xg1_ready, 1)
            pe.wait_ge(pw_ready, 1)

            def up(g, w, ready):
                for k in range(KC):
                    for j in range(4):
                        e = 4 * g + j
                        last = nc.tensor.matmul(up_ps[g][w][32 * j:32 * j + 32, :], xg_T[:, k, e * CAP:(e + 1) * CAP],
                                                wup_sb[:, e, w, k], start=(k == 0), stop=(k == KC - 1))
                last.then_inc(ready, 1)

            def hidden_T(g):
                pe.wait_ge(act_ready, g + 1)
                for k in range(KH):
                    last = nc.tensor.transpose(hT_ps[g][:, k * P:(k + 1) * P], act[:, g, k * P:(k + 1) * P],
                                               ident[:, :])
                last.then_inc(hT_in_psum, 1)

            def down(g):
                pe.wait_ge(hT_ready, g + 1)
                for k in range(KH):
                    for j in range(4):
                        last = nc.tensor.matmul(down_ps[g][32 * j:32 * j + 32, :], h_T[:, g, k, 32 * j:32 * j + 32],
                                                wdn_sb[:, 4 * g + j, k], start=(k == 0), stop=(k == KH - 1))
                last.then_inc(down_in_psum, 1)

            def back_to_tokens(g):
                pe.wait_ge(y_e_ready, g + 1)
                for b in range(TB):
                    last = nc.tensor.matmul(moe_ps[b], scatter[:, g, b], y_e[:, g], start=(g == 0),
                                            stop=(g == EG - 1))
                    if g == EG - 1:
                        last.then_inc(moe_in_psum, 1)

            pe.wait_ge(wup_loaded[0], 16)
            up(0, 0, gate_in_psum)
            up(0, 1, up_in_psum)
            pe.wait_ge(wup_loaded[1], 16)
            up(1, 0, gate_in_psum)
            pe.wait_ge(weighted_ready, 1)
            for g in range(EG):
                for b in range(TB):
                    last = nc.tensor.transpose(scatter_ps[:, g, b], weighted[:, b, g * P:(g + 1) * P], ident[:, :])
            last.then_inc(scatter_in_psum, 1)
            hidden_T(0)
            up(1, 1, up_in_psum)
            pe.wait_ge(wdn_loaded[0], 16)
            down(0)
            pe.wait_ge(scatter_ready, 1)
            hidden_T(1)
            back_to_tokens(0)
            pe.wait_ge(wdn_loaded[1], 16)
            down(1)
            back_to_tokens(1)


def kernel(x, ctx_1024, L0_attn_w_attn, L0_attn_w_proj, L0_ffn_Wg, L0_ffn_W1, L0_ffn_W2, L0_ffn_W3):
    import numpy as np
    import concourse.bacc as bacc
    from concourse.bass_utils import run_bass_kernel_spmd

    def rows(a, n):
        return a.reshape(n, P, -1).transpose(1, 0, 2)

    ctx = np.asarray(ctx_1024)[0]
    w_qkv = np.asarray(L0_attn_w_attn).T
    w_v = w_qkv[:, 2 * C:].reshape(C, NO, 2, 4, HD).transpose(0, 2, 1, 3, 4).reshape(C, C)
    w_proj = np.asarray(L0_attn_w_proj).T.reshape(NO, 2, 4, HD, C).transpose(2, 1, 3, 0, 4).reshape(P, NO, C)
    up = [np.asarray(w).transpose(2, 0, 1).reshape(KC, P, E, H).transpose(1, 2, 0, 3)
          for w in (L0_ffn_W1, L0_ffn_W3)]
    arrays = {
        "x_in": rows(np.asarray(x)[0], TB),
        "ctx_t": ctx.reshape(NCH, CH, KC, P).transpose(0, 3, 2, 1),
        "ctx_v": ctx.reshape(NCH, NT, P, C).transpose(0, 2, 1, 3),
        "w_qkv": rows(np.concatenate([w_qkv[:, :2 * C], w_v], axis=1), KC),
        "w_proj": w_proj,
        "w_gate": rows(np.asarray(L0_ffn_Wg).T, KC),
        "w_up": np.stack(up, axis=2),
        "w_down": np.asarray(L0_ffn_W2).transpose(2, 0, 1).reshape(KH, P, E, C).transpose(1, 2, 0, 3),
    }
    arrays = {k: np.ascontiguousarray(a) for k, a in arrays.items()}
    nc = bacc.Bacc("TRN2", target_bir_lowering=False, num_devices=1)
    aps = [nc.dram_tensor(k, a.shape, mybir.dt.from_np(a.dtype), kind="ExternalInput").ap()
           for k, a in arrays.items()]
    aps.append(nc.dram_tensor("x_out_dram", (P, TB, C), FP32, kind="ExternalOutput").ap())
    build(nc, *aps)
    r = run_bass_kernel_spmd(nc, [arrays], core_ids=[0])
    return r.results[0]["x_out_dram"].transpose(1, 0, 2).reshape(1, T, C)
```
